# Optimizing a Trainium2 kernel written in Bass

```python
import numpy as np
import jax
import jax.numpy as jnp

def _softmax(x, axis=-1):
    return jax.nn.softmax(x, axis=axis)

def _gelu(x):
    return jax.nn.gelu(x, approximate=True)

def _silu(x):
    return jax.nn.silu(x)

def _sigmoid(x):
    return jax.nn.sigmoid(x)

def _layernorm(x, axis=-1, eps=1e-05):
    m = jnp.mean(x, axis=axis, keepdims=True)
    v = jnp.var(x, axis=axis, keepdims=True)
    return (x - m) / jnp.sqrt(v + eps)

def _scatter_add(tgt, idx, src, axis=0):
    return tgt.at[idx].add(src)

def _segment_sum(src, seg, n):
    return jax.ops.segment_sum(src, seg, n)
kernel_name = 'mk_cond_resid_d4_seqx_r4_8c9947'

def setup_inputs(seed: int=0):
    np.random.seed(seed)
    _w = jnp.asarray

    def _rec_inputs():
        import jax
        import jax.numpy as jnp
        _rk = jax.random.key(seed)
        x = 7.22e-05 + 1 * jax.random.normal(jax.random.fold_in(_rk, 1), (16, 256, 256), jnp.float32)
        _lenS = 256 - jax.random.randint(jax.random.fold_in(_rk, 7), (16,), 0, max(1, 256 // 4) + 1, jnp.int32)
        _lenS2 = 256 - jax.random.randint(jax.random.fold_in(_rk, 8), (16,), 0, max(1, 256 // 4) + 1, jnp.int32)
        cond_1024 = 0.00782532 + 1.00527 * jax.random.normal(jax.random.fold_in(_rk, 11), (16, 256), jnp.float32)
        return (x, cond_1024)
    x, cond_1024 = _rec_inputs()

    def _L0_cond_setup():
        import jax, jax.numpy as jnp
        import numpy as np
        EPS = 1e-06
        HEADS = 16

        def _layernorm(x, weight=None):
            mu = jnp.mean(x, axis=-1, keepdims=True)
            var = jnp.var(x, axis=-1, keepdims=True)
            y = (x - mu) / jnp.sqrt(var + EPS)
            return y if weight is None else y * weight

        def _apply_rope(x, position):
            e = x.shape[-1]
            t = x.shape[-2]
            x_rope, x_pass = (x[..., :e // 2], x[..., e // 2:])
            xr = x_rope.reshape(*x_rope.shape[:-1], -1, 2)
            pos = position[:t].reshape(1, 1, t, -1, 2)
            cos, sin = (pos[..., 0], pos[..., 1])
            x0, x1 = (xr[..., 0], xr[..., 1])
            rot = jnp.stack([x0 * cos - x1 * sin, x1 * cos + x0 * sin], axis=-1)
            rot = rot.reshape(*rot.shape[:-2], -1)
            return jnp.concatenate([rot.astype(x.dtype), x_pass], axis=-1)
        key = jax.random.key(seed)
        ks = jax.random.split(key, 8)
        B, T, D, TD = (8, 256, 256, 256)
        e = D // HEADS
        s = 0.02
        return {'x': jax.random.normal(ks[0], (B, T, D), jnp.float32), 'time': jax.random.normal(ks[1], (B, 1, TD), jnp.float32), 'position': jax.random.normal(ks[2], (T, e // 4, 2), jnp.float32), 'mod_w': jax.random.normal(ks[3], (TD, 3 * D), jnp.float32) * s, 'mod_b': jax.random.normal(ks[4], (3 * D,), jnp.float32) * s, 'w_qkv': jax.random.normal(ks[5], (D, 3 * D), jnp.float32) * s, 'w_out': jax.random.normal(ks[6], (D, D), jnp.float32) * s, 'q_norm_w': jnp.ones((e,), jnp.float32), 'k_norm_w': jnp.ones((e,), jnp.float32)}
    _L0_cond_all = _L0_cond_setup()
    _L0_cond_in = {k: v for k, v in _L0_cond_all.items() if k in ('position', 'mod_w', 'mod_b', 'w_qkv', 'w_out', 'q_norm_w', 'k_norm_w')}
    del _L0_cond_all

    def _L1_cond_setup():
        import jax, jax.numpy as jnp
        import numpy as np
        EPS = 1e-08
        key = jax.random.key(seed)
        ks = jax.random.split(key, 8)
        B, S, D, H = (8, 512, 256, 256)
        scale = 1.0 / np.sqrt(D)
        return {'input_seq': jax.random.normal(ks[0], (B, S, D), dtype=jnp.float32), 'initial_hidden': jax.random.normal(ks[1], (B, H), dtype=jnp.float32), 'W_f': jax.random.normal(ks[2], (H, D), dtype=jnp.float32) * scale, 'b_f': jnp.zeros((H,), dtype=jnp.float32), 'W_i': jax.random.normal(ks[3], (H, D), dtype=jnp.float32) * scale, 'b_i': jnp.zeros((H,), dtype=jnp.float32), 'W_h': jax.random.normal(ks[4], (H, D), dtype=jnp.float32) * scale, 'b_h': jnp.zeros((H,), dtype=jnp.float32)}
    _L1_cond_all = _L1_cond_setup()
    _L1_cond_in = {k: v for k, v in _L1_cond_all.items() if k in ('W_f', 'b_f', 'W_i', 'b_i', 'W_h', 'b_h')}
    del _L1_cond_all

    def _L2_cond_setup():
        import jax, jax.numpy as jnp
        import numpy as np
        NUM_EXPERTS = 4
        TOP_K = 2
        key = jax.random.key(seed)
        ks = jax.random.split(key, 16)
        B, L, D, E, H = (8, 192, 256, NUM_EXPERTS, 1024)
        s = 0.02
        return {'context_c': jax.random.normal(ks[0], (B, L, D), jnp.float32), 'time_cond': jax.random.normal(ks[1], (B, D), jnp.float32), 'gate_w': jax.random.normal(ks[2], (3 * D, E), jnp.float32) * s, 'gate_b': jnp.zeros((E,), jnp.float32), 'time_w': jax.random.normal(ks[3], (D, 2 * E), jnp.float32) * s, 'time_b': jnp.zeros((2 * E,), jnp.float32), 'ew1': jax.random.normal(ks[4], (E, D, H), jnp.float32) * s, 'eb1': jnp.zeros((E, H), jnp.float32), 'ew2': jax.random.normal(ks[5], (E, H, D), jnp.float32) * s, 'eb2': jnp.zeros((E, D), jnp.float32), 'sw1': jax.random.normal(ks[6], (D, H), jnp.float32) * s, 'sb1': jnp.zeros((H,), jnp.float32), 'sw2': jax.random.normal(ks[7], (H, D), jnp.float32) * s, 'sb2': jnp.zeros((D,), jnp.float32)}
    _L2_cond_all = _L2_cond_setup()
    _L2_cond_in = {k: v for k, v in _L2_cond_all.items() if k in ('gate_w', 'gate_b', 'time_w', 'time_b', 'ew1', 'eb1', 'ew2', 'eb2', 'sw1', 'sb1', 'sw2', 'sb2')}
    del _L2_cond_all

    def _L3_cond_setup():
        import jax, jax.numpy as jnp
        import numpy as np
        N, T, D, H = (64, 128, 256, 256)
        key = jax.random.key(seed)
        k1, k2, k3, k4 = jax.random.split(key, 4)
        x = jax.random.normal(k1, (N, T, D), dtype=jnp.float32)
        h0 = jax.random.normal(k2, (N, H), dtype=jnp.float32)
        Wx = jax.random.normal(k3, (D, H), dtype=jnp.float32) / jnp.sqrt(jnp.float32(D))
        Wh = jax.random.normal(k4, (H, H), dtype=jnp.float32) / jnp.sqrt(jnp.float32(H))
        b = jnp.zeros((H,), dtype=jnp.float32)
        return {'x': x, 'h0': h0, 'Wx': Wx, 'Wh': Wh, 'b': b}
    _L3_cond_all = _L3_cond_setup()
    _L3_cond_in = {k: v for k, v in _L3_cond_all.items() if k in ('Wx', 'Wh', 'b')}
    del _L3_cond_all
    return {'x': x, 'cond_1024': cond_1024, 'L0_cond_position': _L0_cond_in['position'], 'L0_cond_mod_w': _L0_cond_in['mod_w'], 'L0_cond_mod_b': _L0_cond_in['mod_b'], 'L0_cond_w_qkv': _L0_cond_in['w_qkv'], 'L0_cond_w_out': _L0_cond_in['w_out'], 'L0_cond_q_norm_w': _L0_cond_in['q_norm_w'], 'L0_cond_k_norm_w': _L0_cond_in['k_norm_w'], 'L1_cond_W_f': _L1_cond_in['W_f'], 'L1_cond_b_f': _L1_cond_in['b_f'], 'L1_cond_W_i': _L1_cond_in['W_i'], 'L1_cond_b_i': _L1_cond_in['b_i'], 'L1_cond_W_h': _L1_cond_in['W_h'], 'L1_cond_b_h': _L1_cond_in['b_h'], 'L2_cond_gate_w': _L2_cond_in['gate_w'], 'L2_cond_gate_b': _L2_cond_in['gate_b'], 'L2_cond_time_w': _L2_cond_in['time_w'], 'L2_cond_time_b': _L2_cond_in['time_b'], 'L2_cond_ew1': _L2_cond_in['ew1'], 'L2_cond_eb1': _L2_cond_in['eb1'], 'L2_cond_ew2': _L2_cond_in['ew2'], 'L2_cond_eb2': _L2_cond_in['eb2'], 'L2_cond_sw1': _L2_cond_in['sw1'], 'L2_cond_sb1': _L2_cond_in['sb1'], 'L2_cond_sw2': _L2_cond_in['sw2'], 'L2_cond_sb2': _L2_cond_in['sb2'], 'L3_cond_Wx': _L3_cond_in['Wx'], 'L3_cond_Wh': _L3_cond_in['Wh'], 'L3_cond_b': _L3_cond_in['b']}

def reference(x, cond_1024, L0_cond_position, L0_cond_mod_w, L0_cond_mod_b, L0_cond_w_qkv, L0_cond_w_out, L0_cond_q_norm_w, L0_cond_k_norm_w, L1_cond_W_f, L1_cond_b_f, L1_cond_W_i, L1_cond_b_i, L1_cond_W_h, L1_cond_b_h, L2_cond_gate_w, L2_cond_gate_b, L2_cond_time_w, L2_cond_time_b, L2_cond_ew1, L2_cond_eb1, L2_cond_ew2, L2_cond_eb2, L2_cond_sw1, L2_cond_sb1, L2_cond_sw2, L2_cond_sb2, L3_cond_Wx, L3_cond_Wh, L3_cond_b):
    import jax
    import jax.numpy as jnp

    def _L0_cond_ref(x, time, position, mod_w, mod_b, w_qkv, w_out, q_norm_w, k_norm_w):
        import jax, jax.numpy as jnp
        import numpy as np
        EPS = 1e-06
        HEADS = 16

        def _layernorm(x, weight=None):
            mu = jnp.mean(x, axis=-1, keepdims=True)
            var = jnp.var(x, axis=-1, keepdims=True)
            y = (x - mu) / jnp.sqrt(var + EPS)
            return y if weight is None else y * weight

        def _apply_rope(x, position):
            e = x.shape[-1]
            t = x.shape[-2]
            x_rope, x_pass = (x[..., :e // 2], x[..., e // 2:])
            xr = x_rope.reshape(*x_rope.shape[:-1], -1, 2)
            pos = position[:t].reshape(1, 1, t, -1, 2)
            cos, sin = (pos[..., 0], pos[..., 1])
            x0, x1 = (xr[..., 0], xr[..., 1])
            rot = jnp.stack([x0 * cos - x1 * sin, x1 * cos + x0 * sin], axis=-1)
            rot = rot.reshape(*rot.shape[:-2], -1)
            return jnp.concatenate([rot.astype(x.dtype), x_pass], axis=-1)
        B, T, D = x.shape
        H = HEADS
        e = D // H
        h = _layernorm(x)
        mod = jax.nn.silu(time) @ mod_w + mod_b
        shift, scale, gate = jnp.split(mod, 3, axis=-1)
        h = h * (scale + 1.0) + shift
        qkv = (h @ w_qkv).reshape(B, T, 3, H, e).transpose(2, 0, 3, 1, 4)
        q, k, v = (qkv[0], qkv[1], qkv[2])
        q = _apply_rope(_layernorm(q, q_norm_w), position)
        k = _apply_rope(_layernorm(k, k_norm_w), position)
        scores = jnp.einsum('bhqe,bhke->bhqk', q, k) / jnp.sqrt(jnp.asarray(e, q.dtype))
        attn = jax.nn.softmax(scores, axis=-1)
        o = jnp.einsum('bhqk,bhke->bhqe', attn, v)
        o = o.transpose(0, 2, 1, 3).reshape(B, T, D)
        return o @ w_out * gate

    def _L1_cond_ref(input_seq, initial_hidden, W_f, b_f, W_i, b_i, W_h, b_h):
        import jax, jax.numpy as jnp
        import numpy as np
        EPS = 1e-08
        forget_gate = jax.nn.sigmoid(jnp.einsum('bsd,hd->bsh', input_seq, W_f) + b_f)
        input_gate = jax.nn.sigmoid(jnp.einsum('bsd,hd->bsh', input_seq, W_i) + b_i)
        gate_sum = forget_gate + input_gate + EPS
        forget_norm = forget_gate / gate_sum
        input_norm = input_gate / gate_sum
        candidate = jnp.einsum('bsd,hd->bsh', input_seq, W_h) + b_h
        new_info = input_norm * candidate
        log_ret = jnp.log(forget_norm + EPS)
        log_cumprod = jnp.cumsum(log_ret, axis=1)
        B, _, H = log_cumprod.shape
        padded = jnp.concatenate([jnp.zeros((B, 1, H), dtype=log_cumprod.dtype), log_cumprod], axis=1)
        scaling = jnp.exp(log_cumprod[:, -1:, :] - padded[:, :-1, :])
        hidden = jnp.cumsum(scaling * new_info, axis=1)
        hidden = hidden + jnp.exp(log_cumprod) * initial_hidden[:, None, :]
        return hidden

    def _L2_cond_ref(context_c, time_cond, gate_w, gate_b, time_w, time_b, ew1, eb1, ew2, eb2, sw1, sb1, sw2, sb2):
        import jax, jax.numpy as jnp
        import numpy as np
        NUM_EXPERTS = 4
        TOP_K = 2
        B, L, D = context_c.shape
        E, K = (NUM_EXPERTS, TOP_K)
        L_head = L_wrist = L // 3
        head = context_c[:, :L_head]
        wrist = context_c[:, L_head:L_head + L_wrist]
        proprio = context_c[:, L_head + L_wrist:]
        full_agg = context_c.mean(axis=1)
        hp_agg = jnp.concatenate([head, proprio], axis=1).mean(axis=1)
        wp_agg = jnp.concatenate([wrist, proprio], axis=1).mean(axis=1)
        gate_in = jnp.concatenate([full_agg, hp_agg, wp_agg], axis=-1)
        gate_logits = gate_in @ gate_w + gate_b
        mod = jax.nn.silu(time_cond) @ time_w + time_b
        scale, shift = jnp.split(mod, 2, axis=-1)
        gate_logits = gate_logits * (1.0 + scale) + shift
        gate_scores = jax.nn.softmax(gate_logits, axis=-1)
        topk_w, topk_i = jax.lax.top_k(gate_scores, K)
        topk_w = topk_w / (topk_w.sum(axis=-1, keepdims=True) + 1e-08)
        onehot = (topk_i[..., None] == jnp.arange(E)[None, None, :]).astype(context_c.dtype)
        w_be = jnp.sum(topk_w[..., None] * onehot, axis=1)
        mask = np.ones((E, L), dtype=np.float32)
        mask[1, L_head:L_head + L_wrist] = 0.0
        mask[2, :L_head] = 0.0
        mask = jnp.asarray(mask)
        out = jnp.zeros_like(context_c)
        for e in range(E):
            h = jax.nn.gelu(context_c @ ew1[e] + eb1[e], approximate=True)
            y = h @ ew2[e] + eb2[e]
            out = out + w_be[:, e][:, None, None] * mask[e][None, :, None] * y
        shared = jax.nn.gelu(context_c @ sw1 + sb1, approximate=True) @ sw2 + sb2
        return out + shared

    def _L3_cond_ref(x, h0, Wx, Wh, b):
        import jax, jax.numpy as jnp
        import numpy as np
        N, T, D, H = (64, 128, 256, 256)
        xw = jnp.einsum('ntd,dh->nth', x, Wx) + b

        def step(prev_h, xw_t):
            next_h = jnp.tanh(xw_t + prev_h @ Wh)
            return (next_h, next_h)
        _, hs = jax.lax.scan(step, h0, jnp.swapaxes(xw, 0, 1))
        return jnp.swapaxes(hs, 0, 1)
    x = x + _L0_cond_ref(x, cond_1024[:, None, :], L0_cond_position, L0_cond_mod_w, L0_cond_mod_b, L0_cond_w_qkv, L0_cond_w_out, L0_cond_q_norm_w, L0_cond_k_norm_w)
    x = x + _L1_cond_ref(x, cond_1024, L1_cond_W_f, L1_cond_b_f, L1_cond_W_i, L1_cond_b_i, L1_cond_W_h, L1_cond_b_h)
    x = x + _L2_cond_ref(x, cond_1024, L2_cond_gate_w, L2_cond_gate_b, L2_cond_time_w, L2_cond_time_b, L2_cond_ew1, L2_cond_eb1, L2_cond_ew2, L2_cond_eb2, L2_cond_sw1, L2_cond_sb1, L2_cond_sw2, L2_cond_sb2)
    x = x + _L3_cond_ref(x, cond_1024, L3_cond_Wx, L3_cond_Wh, L3_cond_b)
    return x

_drawn_inputs = setup_inputs


def setup_inputs(seed=0):
    import zlib

    import numpy as np

    out = dict(_drawn_inputs(seed))
    spreads = {'L0_cond_q_norm_w': (1.0, 0.6),
     'L0_cond_k_norm_w': (1.0, 0.6),
     'L1_cond_b_f': (0.0, 2.0),
     'L1_cond_b_i': (0.0, 2.0),
     'L1_cond_b_h': (0.0, 2.0),
     'L2_cond_gate_b': (0.0, 2.0),
     'L2_cond_time_b': (0.0, 0.431),
     'L2_cond_eb1': (0.0, 2.0),
     'L2_cond_eb2': (0.0, 0.8),
     'L2_cond_sb1': (0.0, 2.0),
     'L2_cond_sb2': (0.0, 0.8),
     'L3_cond_b': (0.0, 2.0)}
    factors = {'L0_cond_position': 8.0,
     'L0_cond_mod_w': 7.633,
     'L0_cond_mod_b': 8.0,
     'L0_cond_w_qkv': 7.468,
     'L0_cond_w_out': 7.475,
     'L1_cond_W_f': 5.267,
     'L1_cond_W_i': 5.146,
     'L1_cond_W_h': 2.94,
     'L2_cond_gate_w': 3.48,
     'L3_cond_Wh': 7.872}
    for name, (base, spread) in spreads.items():
        noise = np.random.default_rng([zlib.crc32(name.encode()), seed]).standard_normal(out[name].shape)
        drawn = base * np.exp(spread * noise) if base else spread * noise
        out[name] = jnp.asarray(drawn.astype(out[name].dtype))
    for name, factor in factors.items():
        out[name] = (out[name] * factor).astype(out[name].dtype)
    return out
```

```python
import concourse.bass as bass
from concourse import mybir
from contextlib import ExitStack

P = 128
B, T, D = 16, 256, 256
DC = D // P
TC = T // P
HEADS, HD = 16, 16
HP = HEADS // 2
SLOT = 64
NE, F = 4, 1024
FC = F // P
ROT = HD // 2
SEG = [(0, T // 3), (T // 3, 2 * (T // 3)), (2 * (T // 3), T)]

SMALL = [("mod_b", 6), ("b_f", 2), ("b_i", 2), ("b_h", 2), ("eb1", NE * FC), ("sb1", FC), ("eb2", NE * DC),
         ("sb2", DC), ("rnn_b", DC), ("cond", DC * B), ("qk_w", 2 * HD), ("gate_b", NE), ("time_b", 2 * NE),
         ("gate_w", 3 * DC * NE), ("time_w", DC * 2 * NE), ("pos", TC * ROT), ("rnn_b_row", D)]
SMALL_AT, SMALL_W = {}, 0
for _name, _width in SMALL:
    SMALL_AT[_name] = SMALL_W
    SMALL_W += _width


def later(b):
    return not isinstance(b, int) or b > 0


class Steps:

    def __init__(self, eng, sem, base=0):
        self.eng, self.sem, self.base, self.n, self.last = eng, sem, base, 0, None

    def op(self, ins, sem=None, value=None):
        if sem is None:
            self.n += 1
            sem, value = self.sem, self.base + self.n
        ins.then_inc(sem, 1)
        self.last = (sem, value)

    def fence(self):
        self.eng.wait_ge(*self.last)

    def link(self, ins, sem=None, value=None):
        self.op(ins, sem, value)
        self.fence()


FILLS = ([("scores_max", h) for h in range(HEADS)] + [("max_rows", 0)] + [("scores", h) for h in range(HEADS)]
         + [("out_rows", 0), ("project", 0)] + [("qk_rows", j) for j in range(8)])
ROT_BANKS = 3


def bank_of(fill):
    return FILLS.index(fill) % ROT_BANKS


def fills_before(fill, b):
    n, k = FILLS.index(fill), FILLS.index(fill) % ROT_BANKS
    first = sum(1 for m, f in enumerate(FILLS) if f[0] == "qk_rows" and m % ROT_BANKS == k)
    each = sum(1 for m in range(len(FILLS)) if m % ROT_BANKS == k)
    here = sum(1 for m in range(n) if m % ROT_BANKS == k)
    if fill[0] == "qk_rows":
        return here + first + (b - 1) * each if later(b) else \
            sum(1 for m in range(n) if FILLS[m][0] == "qk_rows" and m % ROT_BANKS == k)
    return first + b * each + here


def last_qk_fill(k, b):
    j = max(j for j in range(8) if bank_of(("qk_rows", j)) == k)
    return fills_before(("qk_rows", j), b) + 1


def build(nc, x_tok, x_dm, small_in, mod_w, w_qkv, w_out, w_fih, ew1, ew2, sw1, sw2, wx, wh, out):
    fp32, fp32r = mybir.dt.float32, mybir.dt.float32r
    ALU, ACT, AX = mybir.AluOpType, mybir.ActivationFunctionType, mybir.AxisListType
    hold = ExitStack()

    def sb(stack, name, shape, dt=fp32):
        return stack.enter_context(nc.sbuf_tensor(name, shape, dt))

    def ps(stack, name, shape):
        return stack.enter_context(nc.psum_tensor(name, shape, fp32))

    def sem(stack, name):
        return stack.enter_context(nc.semaphore(name))

    with hold:
        XT = sb(hold, "XT", [P, DC, B, T])
        small = sb(hold, "small", [P, SMALL_W])
        ident = sb(hold, "ident", [P, P])
        silu = sb(hold, "silu", [P, DC, B])
        eps8 = sb(hold, "eps8", [P, 1])
        wx_sb = sb(hold, "wx_sb", [P, DC, D])
        wh_sb = sb(hold, "wh_sb", [P, DC, D])
        later_loaded = sem(hold, "later_loaded")

        def vec(name, a=None, z=None):
            at = SMALL_AT[name]
            width = dict(SMALL)[name]
            return small[:, at + (a or 0):at + (width if z is None else z)]

        with ExitStack() as early:
            wfih_sb = sb(early, "wfih_sb", [P, DC, 3 * D])
            attention(nc, locals())
            recurrence(nc, locals())
        experts(nc, locals())


def attention(nc, env):
    fp32, fp32r, ALU, ACT, AX = (env[k] for k in ("fp32", "fp32r", "ALU", "ACT", "AX"))
    sb, ps, sem, vec = (env[k] for k in ("sb", "ps", "sem", "vec"))
    XT, small, ident, silu, eps8 = (env[k] for k in ("XT", "small", "ident", "silu", "eps8"))
    st = ExitStack()
    with st:
        xn = sb(st, "xn", [P, B, TC, D])
        wqkv = sb(st, "wqkv", [P, DC, 3 * D])
        wout = sb(st, "wout", [P, DC, D])
        modw = sb(st, "modw", [P, DC, 3 * D])
        modT = sb(st, "modT", [P, 3 * DC, B])
        sig = sb(st, "sig", [P, DC, B])
        stats = sb(st, "stats", [P, B * TC, 6])
        mv = sb(st, "mv", [P, B * TC, 2])
        rstd = sb(st, "rstd", [P, B * TC])
        nmr = sb(st, "nmr", [P, B * TC])
        neghalf = sb(st, "neghalf", [P, 64])
        wmean = sb(st, "wmean", [P, DC, 2 * HEADS])
        ropeA = sb(st, "ropeA", [P, TC, 2, HD])
        ropeB = sb(st, "ropeB", [P, TC, 2, ROT // 2, 2])
        xh = sb(st, "xh", [P, TC, D])
        hT = sb(st, "hT", [P, DC, T])
        sq = sb(st, "sq", [P, TC * 2 * HEADS, HD])
        ssq = sb(st, "ssq", [P, TC * 2 * HEADS])
        rs = sb(st, "rs", [P, TC * 2 * HEADS])
        y = sb(st, "y", [P, TC, 2, HEADS, HD])
        ya = sb(st, "ya", [P, TC, 2, HEADS, HD])
        yb = sb(st, "yb", [P, TC, 2, HEADS, ROT])
        slots = sb(st, "slots", [P, TC, 2, HEADS, SLOT], fp32r)
        QT = sb(st, "QT", [P, 2, HP, T], fp32r)
        KT = sb(st, "KT", [P, 2, HP, T], fp32r)
        vp = sb(st, "vp", [P, 2, TC, HEADS, HD + 2])
        mx = sb(st, "mx", [P, TC, HEADS])
        nm = sb(st, "nm", [P, TC, HEADS], fp32r)
        mT = sb(st, "mT", [HEADS, T], fp32r)
        probs = sb(st, "probs", [P, 4, 2 * T])
        rden = sb(st, "rden", [P, TC, HEADS])
        o = sb(st, "o", [P, TC, D])
        oT = sb(st, "oT", [P, DC, T])

        pA = ps(st, "pA", [P, 3, 512])
        pR = [ps(st, f"pR{k}", [P, 512]) for k in range(ROT_BANKS)]
        pO = ps(st, "pO", [P, TC, 512])

        small_in_s, x_in, w_in, modw_in, xT_in = (sem(st, n) for n in ("small_in_s", "x_in", "w_in", "modw_in", "xT_in"))
        pool_ready, sig_ready, mod_mm, silu_ready, dve_ready, setup_pow, var_ready0 = (
            sem(st, n) for n in ("pool_ready", "sig_ready", "mod_mm", "silu_ready", "dve_ready", "setup_pow", "var_ready0"))
        dve_step, act_step, pool_step = (sem(st, n) for n in ("dve_step", "act_step", "pool_step"))
        xh_ready, x_rows, hT_ready, qkv_done, v_ready, sq_ready, var_ready, rs_ready, y_ready, ya_ready = (
            sem(st, n) for n in ("xh_ready", "x_rows", "hT_ready", "qkv_done", "v_ready", "sq_ready", "var_ready",
                                 "rs_ready", "y_ready", "ya_ready"))
        slots_dve, slots_pool, hi_ready, nm_ready, max_moved, pv_done, o_ready = (
            sem(st, n) for n in ("slots_dve", "slots_pool", "hi_ready", "nm_ready", "max_moved", "pv_done", "o_ready"))
        full = [sem(st, f"full{k}") for k in range(ROT_BANKS)]
        free = [sem(st, f"free{k}") for k in range(ROT_BANKS)]

        slots32 = slots[:].bitcast(fp32)
        qk_psum = pA[:, 1:3, :].rearrange("p t (g e) -> p (t g) e", e=HD)

        def evacuate_qk(eng, copy, b, par, j):
            f = ("qk_rows", j)
            dst = (QT, KT)[j // 4]
            g = j % 4
            eng.wait_ge(full[bank_of(f)], fills_before(f, b) + 1)
            copy(dst[:, par, 2 * g:2 * g + 2], pR[bank_of(f)][:].rearrange("p (h t) -> p h t", h=2)).then_inc(free[bank_of(f)], 1)

        block = st.enter_context(nc.Block())

        @block.sync
        def _(sp):
            sp.dma_start(small[:, :], env["small_in"]).then_inc(small_in_s, 16)
            sp.dma_start(modw[:], env["mod_w"].rearrange("(c p) n -> p c n", p=P)).then_inc(modw_in, 16)
            x_view = env["x_tok"].rearrange("b (c p) d -> p b c d", p=P)
            for q in range(4):
                sp.dma_start(xn[:, 4 * q:4 * q + 4], x_view[:, 4 * q:4 * q + 4]).then_inc(x_in, 16)
            sp.dma_start(wqkv[:], env["w_qkv"].rearrange("(c p) n -> p c n", p=P)).then_inc(w_in, 16)
            sp.dma_start(wout[:], env["w_out"].rearrange("(c p) n -> p c n", p=P)).then_inc(w_in, 16)
            for c in range(DC):
                sp.dma_start(XT[:, c], env["x_dm"][c * P:(c + 1) * P]).then_inc(xT_in, 16)
            later = env["later_loaded"]
            sp.dma_start(env["wfih_sb"][:], env["w_fih"].rearrange("(c p) n -> p c n", p=P)).then_inc(later, 16)
            sp.dma_start(env["wx_sb"][:], env["wx"].rearrange("(c p) n -> p c n", p=P)).then_inc(later, 16)
            sp.dma_start(env["wh_sb"][:], env["wh"].rearrange("(c p) n -> p c n", p=P)).then_inc(later, 16)

            def batch(b, par):
                sp.wait_ge(free[bank_of(("max_rows", 0))], fills_before(("max_rows", 0), b) + 1)
                for s in range(2):
                    row = SLOT * s + 3 * HD
                    sp.dma_start(QT[row:row + 1, par].bitcast(fp32), mT[s * HP:(s + 1) * HP, :].bitcast(fp32)).then_inc(max_moved, 16)
            with sp.Fori(0, B // 2) as i:
                for par in range(2):
                    batch(2 * i + par, par)
            sp.wait_ge(max_moved, 32 * B)

        @block.gpsimd
        def _(pool):
            s = Steps(pool, pool_step)
            s.link(nc.gpsimd.memset(ident[:], 0.0))
            s.op(nc.gpsimd.affine_select(out=ident[:], in_=ident[:], compare_op=ALU.not_equal, fill=1.0, base=0,
                                         pattern=[[-1, P]], channel_multiplier=1))
            s.op(nc.gpsimd.memset(neghalf[:], -0.5))
            s.op(nc.gpsimd.memset(vp[:], 1.0))
            s.op(nc.gpsimd.memset(eps8[:], 1e-8))
            s.link(nc.gpsimd.memset(slots32, 0.0))
            nc.gpsimd.memset(slots32[:, :, 1, :, 3 * HD:3 * HD + 1], 1.0).then_inc(pool_ready, 1)
            pool.wait_ge(pool_ready, 1)
            pool.wait_ge(var_ready0, 1)
            nc.gpsimd.tensor_tensor(rstd[:], rstd[:], neghalf[:, 0:B * TC], ALU.pow).then_inc(setup_pow, 1)

            def prep(b, base):
                s = Steps(pool, pool_step, base)
                pool.wait_ge(var_ready, b + 1)
                if later(b):
                    pool.wait_ge(y_ready, b)
                nc.gpsimd.tensor_tensor(rs[:], ssq[:], neghalf[:], ALU.pow).then_inc(rs_ready, 1)
                pool.wait_ge(y_ready, b + 1)
                if later(b):
                    pool.wait_ge(slots_dve, b)
                for q in range(2):
                    s.op(nc.gpsimd.tensor_tensor(
                        yb[:, :, :, :, q::2].rearrange("p t q h j -> p (t q) h j"),
                        y[:, :, :, :, 1 - q:ROT:2].rearrange("p t q h j -> p (t q) h j"),
                        ropeB[:, :, :, :, q].rearrange("p t q j -> p (t q) j").unsqueeze(2).broadcast_to([P, 2 * TC, HEADS, ROT // 2]),
                        ALU.mult))
                s.link(nc.gpsimd.tensor_tensor(
                    ya[:].rearrange("p t q h e -> p (t q) h e"), y[:].rearrange("p t q h e -> p (t q) h e"),
                    ropeA[:].rearrange("p t q e -> p (t q) e").unsqueeze(2).broadcast_to([P, 2 * TC, HEADS, HD]), ALU.mult))
                yav = ya[:, :, :, :, 0:ROT].rearrange("p t q h j -> p (t q) h j")
                nc.gpsimd.tensor_tensor(yav, yav, yb[:].rearrange("p t q h j -> p (t q) h j"), ALU.add).then_inc(ya_ready, 1)
                pool.wait_ge(hi_ready, b + 1)
                s.op(nc.gpsimd.tensor_tensor(slots[:, :, 0, :, HD:2 * HD], ya[:, :, 0], slots32[:, :, 0, :, 0:HD], ALU.subtract))
                s.op(nc.gpsimd.tensor_tensor(slots[:, :, 1, :, 2 * HD:3 * HD], ya[:, :, 1], slots32[:, :, 1, :, 0:HD], ALU.subtract),
                     slots_pool, b + 1)
                assert s.n == 4, s.n

            prep(0, 6)
            with pool.Fori(0, B // 2 - 1) as i:
                prep(2 * i + 1, 6 + 4 * (2 * i + 1))
                prep(2 * i + 2, 6 + 4 * (2 * i + 2))
            prep(B - 1, 6 + 4 * (B - 1))

        @block.scalar
        def _(act):
            act.wait_ge(small_in_s, 16)
            nc.scalar.activation(sig[:].rearrange("p c b -> p (c b)"), vec("cond"), ACT.Sigmoid).then_inc(sig_ready, 1)

            def prep1(b, par):
                act.wait_ge(x_rows, b + 1)
                if not later(b):
                    act.wait_ge(dve_ready, 1)
                else:
                    act.wait_ge(qkv_done, b)
                s = Steps(act, act_step, b)
                for c in range(DC):
                    i = nc.scalar.activation(hT[:, c], pA[:, 0, c * T:(c + 1) * T], ACT.Identity,
                                             bias=modT[:, c, bass.ds(b, 1)], scale=modT[:, DC + c, bass.ds(b, 1)])
                    s.op(i) if c == 0 else s.op(i, hT_ready, b + 1)

            def prep2(b, par):
                act.wait_ge(qkv_done, b + 1)
                if later(b):
                    act.wait_ge(var_ready, b)
                nc.scalar.activation(sq[:], qk_psum, ACT.Square).then_inc(sq_ready, 1)
                if not later(b):
                    act.wait_ge(pool_ready, 1)
                nc.scalar.activation(vp[:, par, :, :, 0:HD], pA[:, 0, :].rearrange("p (c h e) -> p c h e", c=TC, e=HD),
                                     ACT.Copy).then_inc(v_ready, 1)

            def prep3(b, par):
                for j in range(0, 8, 2):
                    evacuate_qk(act, nc.scalar.copy, b, par, j)

            def attend(b, par, bn, parn):
                if bn is not None:
                    prep1(bn, parn)
                    prep2(bn, parn)
                f = ("max_rows", 0)
                act.wait_ge(full[bank_of(f)], fills_before(f, b) + 1)
                act.wait_ge(max_moved, 32 * b)
                nc.scalar.copy(mT[:, :], pR[bank_of(f)][0:HEADS, 0:T]).then_inc(free[bank_of(f)], 1)
                for h in range(HEADS):
                    f = ("scores", h)
                    act.wait_ge(full[bank_of(f)], fills_before(f, b) + 1)
                    act.wait_ge(pv_done, HEADS * b + max(h - 3, 0))
                    nc.scalar.activation(probs[:, h % 4], pR[bank_of(f)][:], ACT.Exp, scale=HD ** -0.5).then_inc(free[bank_of(f)], 1)
                f = ("out_rows", 0)
                act.wait_ge(full[bank_of(f)], fills_before(f, b) + 1)
                nc.scalar.copy(oT[:].rearrange("p c t -> p (c t)"), pR[bank_of(f)][:]).then_inc(free[bank_of(f)], 1)
                if bn is not None:
                    prep3(bn, parn)

            prep1(0, 0)
            prep2(0, 0)
            prep3(0, 0)
            with act.Fori(0, B // 2 - 1) as i:
                attend(2 * i, 0, 2 * i + 1, 1)
                attend(2 * i + 1, 1, 2 * i + 2, 0)
            attend(B - 2, 0, B - 1, 1)
            attend(B - 1, 1, None, None)

        @block.vector
        def _(dve):
            s = Steps(dve, dve_step)
            dve.wait_ge(small_in_s, 16)
            dve.wait_ge(sig_ready, 1)
            nc.vector.tensor_tensor(silu[:].rearrange("p c b -> p (c b)"), sig[:].rearrange("p c b -> p (c b)"),
                                    vec("cond"), ALU.mult).then_inc(silu_ready, 1)
            for q in range(4):
                dve.wait_ge(x_in, 64)
                for n in range(8 * q, 8 * q + 8):
                    s.op(nc.vector.bn_stats(stats[:, n], xn[:, n // TC, n % TC]))
            s.fence()
            for n in range(B * TC):
                s.op(nc.vector.bn_aggr(mv[:, n], stats[:, n]))
            s.fence()
            nc.vector.tensor_scalar(rstd[:], mv[:, :, 1], 1e-6, None, ALU.add).then_inc(var_ready0, 1)
            dve.wait_ge(w_in, 32)
            qk_w = wqkv[:, :, 0:2 * D].rearrange("p c (g e) -> p c g e", e=HD)
            s.link(nc.vector.reduce_sum(wmean[:], qk_w, AX.X))
            s.link(nc.vector.tensor_scalar(wmean[:], wmean[:], -1.0 / HD, None, ALU.mult))
            s.op(nc.vector.tensor_tensor(qk_w, qk_w, wmean[:].unsqueeze(3).broadcast_to([P, DC, 2 * HEADS, HD]), ALU.add))
            w2 = vec("qk_w").rearrange("p (q e) -> p q e", q=2)
            pos = vec("pos").rearrange("p (t j i) -> p t j i", t=TC, i=2)
            wr = w2[:, :, 0:ROT].rearrange("p q (j i) -> p q j i", i=2)
            for t in range(TC):
                cos = pos[:, t, :, 0].unsqueeze(1).unsqueeze(3).broadcast_to([P, 2, ROT // 2, 2])
                sin = pos[:, t, :, 1].unsqueeze(1).broadcast_to([P, 2, ROT // 2])
                s.op(nc.vector.tensor_tensor(ropeA[:, t, :, 0:ROT].rearrange("p q (j i) -> p q j i", i=2), wr, cos, ALU.mult))
                s.op(nc.vector.tensor_copy(ropeA[:, t, :, ROT:HD], w2[:, :, ROT:HD]))
                s.op(nc.vector.scalar_tensor_tensor(out=ropeB[:, t, :, :, 0], in0=wr[:, :, :, 1], scalar=-1.0, in1=sin,
                                                    op0=ALU.mult, op1=ALU.mult))
                s.op(nc.vector.tensor_tensor(ropeB[:, t, :, :, 1], wr[:, :, :, 0], sin, ALU.mult))
            dve.wait_ge(mod_mm, 1)
            s.link(nc.vector.tensor_tensor(modT[:], pA[:, 0, 0:3 * DC * B].rearrange("p (m b) -> p m b", b=B),
                                           vec("mod_b").unsqueeze(2).broadcast_to([P, 3 * DC, B]), ALU.add))
            s.op(nc.vector.tensor_scalar(modT[:, DC:2 * DC], modT[:, DC:2 * DC], 1.0, None, ALU.add), dve_ready, 1)
            dve.wait_ge(dve_ready, 1)
            dve.wait_ge(setup_pow, 1)
            s.link(nc.vector.scalar_tensor_tensor(out=nmr[:], in0=mv[:, :, 0], scalar=-1.0, in1=rstd[:],
                                                  op0=ALU.mult, op1=ALU.mult))
            BASE = s.n

            def prep1(b):
                if later(b):
                    dve.wait_ge(x_rows, b)
                for t in range(TC):
                    n = TC * b + t
                    nc.vector.tensor_scalar(xh[:, t], xn[:, bass.ds(b, 1), t].rearrange("p o d -> p (o d)"),
                                            rstd[:, bass.ds(n, 1)], nmr[:, bass.ds(n, 1)], ALU.mult, ALU.add).then_inc(xh_ready, 1)

            def prep2(b, base):
                s = Steps(dve, dve_step, base)
                dve.wait_ge(sq_ready, b + 1)
                s.link(nc.vector.reduce_sum(ssq[:], sq[:], AX.X))
                s.op(nc.vector.tensor_scalar(ssq[:], ssq[:], 1.0 / HD, 1e-6, ALU.mult, ALU.add), var_ready, b + 1)
                dve.wait_ge(rs_ready, b + 1)
                if later(b):
                    dve.wait_ge(slots_pool, b)
                s.op(nc.vector.tensor_tensor(y[:].rearrange("p t q h e -> p (t q h) e"), qk_psum,
                                             rs[:].unsqueeze(2).broadcast_to([P, TC * 2 * HEADS, HD]), ALU.mult), y_ready, b + 1)
                dve.wait_ge(ya_ready, b + 1)
                if later(b):
                    for k in range(ROT_BANKS):
                        dve.wait_ge(full[k], last_qk_fill(k, b - 1))
                else:
                    dve.wait_ge(pool_ready, 1)
                s.op(nc.vector.tensor_copy(slots[:, :, :, :, 0:HD].rearrange("p t q h e -> p (t q) h e"),
                                           ya[:].rearrange("p t q h e -> p (t q) h e")), hi_ready, b + 1)
                s.op(nc.vector.tensor_copy(slots[:, :, 0, :, 2 * HD:3 * HD], ya[:, :, 0]))
                s.op(nc.vector.tensor_copy(slots[:, :, 1, :, HD:2 * HD], ya[:, :, 1]), slots_dve, b + 1)
                assert s.n == 2, s.n

            def prep3(b, par):
                for j in range(1, 8, 2):
                    evacuate_qk(dve, nc.vector.tensor_copy, b, par, j)

            STEP = 4

            def attend(b, par, bn, parn):
                if bn is not None:
                    prep1(bn)
                for h in range(HEADS):
                    f = ("scores_max", h)
                    dve.wait_ge(full[bank_of(f)], fills_before(f, b) + 1)
                    nc.vector.reduce_max(mx[:, :, h], pR[bank_of(f)][:].rearrange("p (c k) -> p c k", c=TC), AX.X)\
                        .then_inc(free[bank_of(f)], 1)
                for k in range(ROT_BANKS):
                    h = max(h for h in range(HEADS) if bank_of(("scores_max", h)) == k)
                    dve.wait_ge(free[k], fills_before(("scores_max", h), b) + 1)
                nc.vector.tensor_scalar(nm[:].rearrange("p c (s g) -> p c g s", s=2), mx[:].rearrange("p c (g s) -> p c g s", s=2),
                                        -1.0, None, ALU.mult).then_inc(nm_ready, 1)
                base = BASE + 2 + STEP * b
                if bn is not None:
                    prep2(bn, base)
                dve.wait_ge(pv_done, HEADS * (b + 1))
                pv = pO[:, :, 0:HEADS * (HD + 1)].rearrange("p c (h e) -> p c h e", e=HD + 1)
                s = Steps(dve, dve_step, base + (2 if bn is not None else 0))
                s.link(nc.vector.reciprocal(rden[:], pv[:, :, :, HD]))
                s.op(nc.vector.tensor_tensor(o[:].rearrange("p c (h e) -> p c h e", e=HD), pv[:, :, :, 0:HD],
                                             rden[:].unsqueeze(3).broadcast_to([P, TC, HEADS, HD]), ALU.mult), o_ready, b + 1)
                f = ("project", 0)
                dve.wait_ge(full[bank_of(f)], fills_before(f, b) + 1)
                dve.wait_ge(xT_in, 32)
                for c in range(DC):
                    xv = XT[:, c, bass.ds(b, 1)].rearrange("p o t -> p (o t)")
                    i = nc.vector.scalar_tensor_tensor(out=xv, in0=pR[bank_of(f)][:, c * T:(c + 1) * T],
                                                       scalar=modT[:, 2 * DC + c, bass.ds(b, 1)], in1=xv, op0=ALU.mult, op1=ALU.add)
                    s.op(i) if c == 0 else s.op(i, free[bank_of(f)], fills_before(f, b) + 1)
                if bn is not None:
                    prep3(bn, parn)
                assert s.n == 2, s.n

            prep1(0)
            prep2(0, BASE)
            prep3(0, 0)
            with dve.Fori(0, B // 2 - 1) as i:
                attend(2 * i, 0, 2 * i + 1, 1)
                attend(2 * i + 1, 1, 2 * i + 2, 0)
            attend(B - 2, 0, B - 1, 1)
            attend(B - 1, 1, None, None)

        @block.tensor
        def _(pe):
            pe.wait_ge(silu_ready, 1)
            pe.wait_ge(modw_in, 16)
            for m in range(3 * DC):
                for c in range(DC):
                    i = nc.tensor.matmul(pA[:, 0, m * B:(m + 1) * B], modw[:, c, m * P:(m + 1) * P], silu[:, c],
                                         start=(c == 0), stop=(c == DC - 1))
            i.then_inc(mod_mm, 1)

            def filling(f, b):
                k = bank_of(f)
                if not isinstance(b, int) or fills_before(f, b) > 0:
                    pe.wait_ge(free[k], fills_before(f, b))
                return pR[k], full[k]

            def rows_of_x(b):
                pe.wait_ge(xh_ready, TC * (b + 1))
                if not later(b):
                    pe.wait_ge(dve_ready, 1)
                    pe.wait_ge(pool_ready, 1)
                else:
                    pe.wait_ge(v_ready, b)
                for c in range(DC):
                    for t in range(TC):
                        i = nc.tensor.transpose(pA[:, 0, c * T + t * P:c * T + (t + 1) * P], xh[:, t, c * P:(c + 1) * P], ident[:])
                i.then_inc(x_rows, 1)

            def qkv(b):
                pe.wait_ge(hT_ready, b + 1)
                if later(b):
                    pe.wait_ge(y_ready, b)
                for t in range(TC):
                    for dst, a, z in ((pA[:, 1 + t, :], 0, 2 * D), (pA[:, 0, t * D:(t + 1) * D], 2 * D, 3 * D)):
                        for c in range(DC):
                            i = nc.tensor.matmul(dst, hT[:, c, t * P:(t + 1) * P], wqkv[:, c, a:z], start=(c == 0), stop=(c == DC - 1))
                i.then_inc(qkv_done, 1)

            def rows_of_qk(b):
                pe.wait_ge(slots_dve, b + 1)
                pe.wait_ge(slots_pool, b + 1)
                for j in range(8):
                    bank, done = filling(("qk_rows", j), b)
                    for g in range(2):
                        for t in range(TC):
                            h = 2 * (2 * (j % 4) + g)
                            i = nc.tensor.transpose(bank[:, g * T + t * P:g * T + (t + 1) * P],
                                                    slots32[:, t, j // 4, h:h + 2].rearrange("p h e -> p (h e)"), ident[:])
                    i.then_inc(done, 1)

            def attend(b, par, bn):
                for k in range(ROT_BANKS):
                    pe.wait_ge(free[k], last_qk_fill(k, b))
                for h in range(HEADS):
                    lo, g = SLOT * (h % 2), h // 2
                    if bn is not None and h == 4:
                        rows_of_x(bn)
                    if bn is not None and h == 10:
                        qkv(bn)
                    bank, done = filling(("scores_max", h), b)
                    for t in range(TC):
                        i = nc.tensor.matmul(bank[:, t * T:(t + 1) * T], QT[lo:lo + 3 * HD, par, g, t * P:(t + 1) * P],
                                             KT[lo:lo + 3 * HD, par, g], start=True, stop=True)
                    i.then_inc(done, 1)
                bank, done = filling(("max_rows", 0), b)
                pe.wait_ge(nm_ready, b + 1)
                for t in range(TC):
                    i = nc.tensor.transpose(bank[0:HEADS, t * P:(t + 1) * P], nm[:, t].bitcast(fp32), ident[:])
                i.then_inc(done, 1)

                def values(h):
                    f = ("scores", h)
                    pe.wait_ge(free[bank_of(f)], fills_before(f, b) + 1)
                    for t in range(TC):
                        for c in range(TC):
                            i = nc.tensor.matmul(pO[:, t, h * (HD + 1):(h + 1) * (HD + 1)],
                                                 probs[:, h % 4, c * T + t * P:c * T + (t + 1) * P],
                                                 vp[:, par, c, h, 0:HD + 1], start=(c == 0), stop=(c == TC - 1))
                    i.then_inc(pv_done, 1)
                pe.wait_ge(max_moved, 32 * (b + 1))
                pe.wait_ge(o_ready, b)
                pe.wait_ge(v_ready, b + 1)
                for h in range(HEADS):
                    lo, g = SLOT * (h % 2), h // 2
                    bank, done = filling(("scores", h), b)
                    for c in range(TC):
                        i = nc.tensor.matmul(bank[:, c * T:(c + 1) * T], KT[lo:lo + 3 * HD + 1, par, g, c * P:(c + 1) * P],
                                             QT[lo:lo + 3 * HD + 1, par, g], start=True, stop=True)
                    i.then_inc(done, 1)
                    if h >= 2:
                        values(h - 2)
                values(HEADS - 2)
                values(HEADS - 1)
                bank, done = filling(("out_rows", 0), b)
                pe.wait_ge(o_ready, b + 1)
                for c in range(DC):
                    for t in range(TC):
                        i = nc.tensor.transpose(bank[:, c * T + t * P:c * T + (t + 1) * P], o[:, t, c * P:(c + 1) * P], ident[:])
                i.then_inc(done, 1)
                bank, done = filling(("project", 0), b)
                pe.wait_ge(free[bank_of(("out_rows", 0))], fills_before(("out_rows", 0), b) + 1)
                for m in range(DC):
                    for c in range(DC):
                        i = nc.tensor.matmul(bank[:, m * T:(m + 1) * T], wout[:, c, m * P:(m + 1) * P], oT[:, c],
                                             start=(c == 0), stop=(c == DC - 1))
                i.then_inc(done, 1)
                if bn is not None:
                    rows_of_qk(bn)

            rows_of_x(0)
            qkv(0)
            rows_of_qk(0)
            with pe.Fori(0, B // 2 - 1) as i:
                attend(2 * i, 0, 2 * i + 1)
                attend(2 * i + 1, 1, 2 * i + 2)
            attend(B - 2, 0, B - 1)
            attend(B - 1, 1, None)


def recurrence(nc, env):
    fp32, ALU, ACT = (env[k] for k in ("fp32", "ALU", "ACT"))
    sb, ps, sem, vec = (env[k] for k in ("sb", "ps", "sem", "vec"))
    XT, eps8, wfih = (env[k] for k in ("XT", "eps8", "wfih_sb"))
    N = 2 * T
    st = ExitStack()
    with st:
        zeros = sb(st, "zeros", [P, T])
        fg = sb(st, "fg", [P, 2, N])
        ig = sb(st, "ig", [P, 2, N])
        total = sb(st, "total", [P, 2, N])
        inv = sb(st, "inv", [P, 2, N])
        new = sb(st, "new", [P, 2, N])
        logs = sb(st, "logs", [P, 2, 2, T + 1])
        scaling = sb(st, "scaling", [P, 2, N])
        decay = sb(st, "decay", [P, 2, N])
        hid = sb(st, "hid", [P, 2, N])
        pg = [ps(st, f"pg{u}", [P, 3, N]) for u in range(2)]
        dve_step, pool_step, act_step = (sem(st, n) for n in ("dve_step2", "pool_step2", "act_step2"))
        zeros_ready = sem(st, "zeros_ready")
        products, gates, summed, inverse, normed, log_ready, cum, scales, hid_ready, added, mult_done, run_done = (
            [sem(st, f"{n}{u}") for u in range(2)] for n in
            ("products", "gates", "summed", "inverse", "normed", "log_ready", "cum", "scales", "hid_ready", "added",
             "mult_done", "run_done"))
        block = st.enter_context(nc.Block())
        PAIRS = B // 2


        @block.tensor
        def _(pe):
            pe.wait_ge(env["later_loaded"], 48)

            def unit(p, u):
                pe.wait_ge(gates[u], 2 * p)
                pe.wait_ge(cum[u], 2 * p)
                for g in range(3):
                    for c in range(DC):
                        i = nc.tensor.matmul(pg[u][:, g], wfih[:, c, g * D + u * P:g * D + (u + 1) * P],
                                             XT[:, c, bass.ds(2 * p, 2)], start=(c == 0), stop=(c == DC - 1))
                i.then_inc(products[u], 1)
            with pe.Fori(0, PAIRS) as p:
                unit(p, 0)
                unit(p, 1)

        def flow(eng, first, second, third):
            first(0, 0)
            with eng.Fori(0, PAIRS - 1) as p:
                second(p, 0)
                first(p, 1)
                third(p, 0)
                second(p, 1)
                first(p + 1, 0)
                third(p, 1)
            second(PAIRS - 1, 0)
            first(PAIRS - 1, 1)
            third(PAIRS - 1, 0)
            second(PAIRS - 1, 1)
            third(PAIRS - 1, 1)

        @block.scalar
        def _(act):
            def first(p, u):
                act.wait_ge(products[u], p + 1)
                act.wait_ge(normed[u], 2 * p)
                act.wait_ge(log_ready[u], p)
                nc.scalar.activation(fg[:, u], pg[u][:, 0], ACT.Sigmoid, bias=vec("b_f", u, u + 1)).then_inc(gates[u], 1)
                nc.scalar.activation(ig[:, u], pg[u][:, 1], ACT.Sigmoid, bias=vec("b_i", u, u + 1)).then_inc(gates[u], 1)

            def second(p, u):
                act.wait_ge(normed[u], 2 * p + 1)
                nc.scalar.activation(fg[:, u], fg[:, u], ACT.Ln, bias=eps8[:, 0:1]).then_inc(log_ready[u], 1)

            def third(p, u):
                act.wait_ge(cum[u], 2 * p + 2)
                act.wait_ge(hid_ready[u], p)
                for j in range(2):
                    nc.scalar.activation(scaling[:, u, j * T:(j + 1) * T], logs[:, u, j, 0:T], ACT.Exp,
                                         bias=logs[:, u, j, T:T + 1], scale=-1.0).then_inc(act_step, 1)
                nc.scalar.activation(decay[:, u].rearrange("p (j t) -> p j t", j=2), logs[:, u, :, 1:T + 1], ACT.Exp).then_inc(scales[u], 1)
            flow(act, first, second, third)

        @block.gpsimd
        def _(pool):
            def first(p, u):
                pool.wait_ge(gates[u], 2 * p + 2)
                s = Steps(pool, pool_step, 2 * p + u)
                s.link(nc.gpsimd.tensor_tensor(total[:, u], fg[:, u], ig[:, u], ALU.add))
                nc.gpsimd.tensor_tensor(total[:, u], total[:, u], eps8[:, 0:1].broadcast_to([P, N]), ALU.add).then_inc(summed[u], 1)

            def second(p, u):
                pool.wait_ge(inverse[u], p + 1)
                nc.gpsimd.tensor_tensor(fg[:, u], fg[:, u], inv[:, u], ALU.mult).then_inc(normed[u], 1)
                nc.gpsimd.tensor_tensor(ig[:, u], ig[:, u], inv[:, u], ALU.mult).then_inc(normed[u], 1)

            def third(p, u):
                pool.wait_ge(hid_ready[u], p + 1)
                pool.wait_ge(products[1], p + 1)
                xv = XT[:, u, bass.ds(2 * p, 2)]
                nc.gpsimd.tensor_tensor(xv, xv, hid[:, u].rearrange("p (j t) -> p j t", j=2), ALU.add).then_inc(added[u], 1)
            flow(pool, first, second, third)

        @block.vector
        def _(dve):
            nc.vector.memset(logs[:, :, :, 0:1], 0.0).then_inc(zeros_ready, 1)
            nc.vector.memset(zeros[:], 0.0).then_inc(zeros_ready, 1)
            dve.wait_ge(zeros_ready, 2)

            def first(p, u):
                dve.wait_ge(summed[u], p + 1)
                dve.wait_ge(normed[u], 2 * p)
                nc.vector.reciprocal(inv[:, u], total[:, u]).then_inc(inverse[u], 1)

            def second(p, u):
                dve.wait_ge(log_ready[u], p + 1)
                dve.wait_ge(normed[u], 2 * p + 2)
                dve.wait_ge(scales[u], p)
                nc.vector.scalar_tensor_tensor(out=new[:, u], in0=pg[u][:, 2], scalar=vec("b_h", u, u + 1), in1=ig[:, u],
                                               op0=ALU.add, op1=ALU.mult).then_inc(dve_step, 1)
                for j in range(2):
                    nc.vector.tensor_tensor_scan(logs[:, u, j, 1:T + 1], fg[:, u, j * T:(j + 1) * T], zeros[:], 0.0,
                                                 ALU.add, ALU.add).then_inc(cum[u], 1)

            def third(p, u):
                dve.wait_ge(scales[u], p + 1)
                dve.wait_ge(added[u], p)
                i = nc.vector.tensor_tensor(new[:, u], scaling[:, u], new[:, u], ALU.mult)
                i.then_inc(mult_done[u], 1)
                dve.wait_ge(mult_done[u], p + 1)
                for j in range(2):
                    nc.vector.tensor_tensor_scan(hid[:, u, j * T:(j + 1) * T], new[:, u, j * T:(j + 1) * T], zeros[:], 0.0,
                                                 ALU.add, ALU.add).then_inc(run_done[u], 1)
                dve.wait_ge(run_done[u], 2 * p + 2)
                for j in range(2):
                    i = nc.vector.scalar_tensor_tensor(
                        out=hid[:, u, j * T:(j + 1) * T], in0=decay[:, u, j * T:(j + 1) * T],
                        scalar=vec("cond").rearrange("p (c b) -> p c b", c=DC)[:, u, bass.ds(2 * p + j, 1)],
                        in1=hid[:, u, j * T:(j + 1) * T], op0=ALU.mult, op1=ALU.add)
                    i.then_inc((dve_step, hid_ready[u])[j], 1)
            flow(dve, first, second, third)


JOBS = {
    0: [(0, 2, 0, T, 0, T), (2, 2, 0, T, 0, T)],
    1: [(0, 4, 0, SEG[0][1] + 1, 0, SEG[0][1]), (0, 4, SEG[2][0], T, SEG[2][0], T)],
    2: [(0, 2, SEG[1][0] - 1, T, SEG[1][0], T), (2, 2, SEG[1][0] - 1, T, SEG[1][0], T)],
    3: [(0, 2, 0, T, 0, T), (2, 2, 0, T, 0, T)],
}
KEPT = [[0, 1, 3], [0, 2, 3], [0, 1, 2, 3]]
CH = 32
NCH = T // CH


def experts(nc, env):
    fp32, fp32r, ALU, ACT, AX = (env[k] for k in ("fp32", "fp32r", "ALU", "ACT", "AX"))
    sb, ps, sem, vec = (env[k] for k in ("sb", "ps", "sem", "vec"))
    XT, silu = env["XT"], env["silu"]
    st = ExitStack()
    with st:
        xhi = sb(st, "xhi", [P, DC, B, T], fp32r)
        xlo = sb(st, "xlo", [P, DC, B, T], fp32r)
        w1 = sb(st, "w1", [P, 2, 2, DC, F], fp32r)
        w2 = sb(st, "w2", [P, 2, 2, FC, D], fp32r)
        g = sb(st, "g", [P, 2, 2 * T])
        ghi = sb(st, "ghi", [P, 2, 2 * T], fp32r)
        glo = sb(st, "glo", [P, 2, 2 * T], fp32r)
        dve_step, pool_step = sem(st, "dve_step3"), sem(st, "pool_step3")
        w_split = sem(st, "w_split")
        up_done, gelu_done, hi_done, lo_done, down_done = ([sem(st, f"{n}{q}") for q in range(2)] for n in
                                                           ("up_done", "gelu_done", "hi_done", "lo_done", "down_done"))
        y_free = sem(st, "y_free")

        def products(pe, dst, whi, wlo, hi, lo, first, last):
            out = []
            for n, (w, x) in enumerate(((whi, hi), (whi, lo), (wlo, hi))):
                out.append(lambda w=w, x=x, n=n: nc.tensor.matmul(dst, w, x, start=(first and n == 0), stop=(last and n == 2)))
            return out

        def up(pe, ph, buf, f, xs, n):
            out = []
            for c in range(DC):
                w = [w1[:, buf, k, c, f * P:(f + 1) * P] for k in range(2)]
                out += products(pe, ph[f % 2][:, 0:n], w[0], w[1], xhi[:, c][xs], xlo[:, c][xs], c == 0, c == DC - 1)
            return out

        def down(pe, py, buf, f, n):
            out = []
            for m in range(DC):
                w = [w2[:, buf, k, f, m * P:(m + 1) * P] for k in range(2)]
                out += products(pe, py[:, m, 0:n], w[0], w[1], ghi[:, f % 2, 0:n], glo[:, f % 2, 0:n], f == 0, f == FC - 1)
            return out

        def split_hidden(dve, f, m, n):
            q = f % 2
            dve.wait_ge(gelu_done[q], m + 1)
            dve.wait_ge(down_done[q], m)
            nc.vector.tensor_copy(ghi[:, q, 0:n], g[:, q, 0:n]).then_inc(hi_done[q], 1)
            dve.wait_ge(hi_done[q], m + 1)
            nc.vector.tensor_tensor(glo[:, q, 0:n], g[:, q, 0:n], ghi[:, q, 0:n].bitcast(fp32), ALU.subtract).then_inc(lo_done[q], 1)

        def gelu(act, ph, bias, f, m, n):
            q = f % 2
            act.wait_ge(up_done[q], m + 1)
            act.wait_ge(lo_done[q], m)
            nc.scalar.activation(g[:, q, 0:n], ph[q][:, 0:n], ACT.Gelu_apprx_tanh, bias=bias).then_inc(gelu_done[q], 1)

        with ExitStack() as routed:
            raw1 = sb(routed, "raw1", [P, DC, F])
            raw2 = sb(routed, "raw2", [P, FC, D])
            segs = sb(routed, "segs", [P, 3, DC, B])
            agg = sb(routed, "agg", [P, 3, DC, B])
            prod = sb(routed, "prod", [P, 3 * DC, B, NE])
            prod2 = sb(routed, "prod2", [P, DC, B, 2 * NE])
            ones = sb(routed, "ones", [P, P])
            earlier = sb(routed, "earlier", [P, NE, NE])
            lg = sb(routed, "lg", [P, B, NE])
            md = sb(routed, "md", [P, B, 2 * NE])
            red = sb(routed, "red", [P, B])
            gt = sb(routed, "gt", [P, B, NE, NE])
            eq = sb(routed, "eq", [P, B, NE, NE])
            we = sb(routed, "we", [P, B, NE])
            bt = sb(routed, "bt", [P, DC, B, 3])
            ph = [ps(routed, f"ph{q}", [P, 512]) for q in range(2)]
            py = [ps(routed, f"py{q}", [P, DC, 512]) for q in range(2)]
            pgate = ps(routed, "pgate", [P, B * NE])
            ptime = ps(routed, "ptime", [P, 2 * NE * B])
            raw_in1, raw_in2, raw_used1, raw_used2, hi_copied = (sem(routed, n) for n in
                                                                 ("raw_in1", "raw_in2", "raw_used1", "raw_used2", "hi_copied"))
            gate_in, gate_mm, exp_in, exp_done, x_hi, x_split, tables = (
                sem(routed, n) for n in ("gate_in", "gate_mm", "exp_in", "exp_done", "x_hi", "x_split", "tables"))
            w_used = sem(routed, "w_used")
            block = routed.enter_context(nc.Block())
            ROUNDS = 4

            @block.sync
            def _(sp):
                for e in range(NE + 1):
                    a, b = (env["ew1"][e], env["ew2"][e]) if e < NE else (env["sw1"], env["sw2"])
                    if e > 0:
                        sp.wait_ge(raw_used1, 2 * e)
                    sp.dma_start(raw1[:], a.rearrange("(c p) f -> p c f", p=P)).then_inc(raw_in1, 16)
                    if e > 0:
                        sp.wait_ge(raw_used2, 2 * e)
                    sp.dma_start(raw2[:], b.rearrange("(c p) d -> p c d", p=P)).then_inc(raw_in2, 16)

            @block.gpsimd
            def _(pool):
                nc.gpsimd.memset(ones[:], 1.0).then_inc(tables, 1)
                nc.gpsimd.memset(earlier[:], 0.0).then_inc(tables, 1)
                pool.wait_ge(tables, 2)
                for e in range(1, NE):
                    nc.gpsimd.memset(earlier[:, e, 0:e], 1.0).then_inc(tables, 1)

                def split_weights(e):
                    for w, raw, arrived, used in ((w1, raw1, raw_in1, raw_used1), (w2, raw2, raw_in2, raw_used2)):
                        pool.wait_ge(arrived, 16 * (e + 1))
                        if e >= 2:
                            pool.wait_ge(w_used, e - 1)
                        nc.gpsimd.tensor_copy(w[:, e % 2, 0], raw[:]).then_inc(used, 1)
                        pool.wait_ge(used, 2 * e + 1)
                        nc.gpsimd.tensor_tensor(w[:, e % 2, 1], raw[:], w[:, e % 2, 0].bitcast(fp32), ALU.subtract).then_inc(used, 1)
                    pool.wait_ge(raw_used1, 2 * e + 2)
                    pool.wait_ge(raw_used2, 2 * e + 2)
                    pool.sem_inc(w_split, 1)

                split_weights(0)
                for c in range(DC):
                    pool.wait_ge(x_hi, c + 1)
                    nc.gpsimd.tensor_tensor(xlo[:, c], XT[:, c], xhi[:, c].bitcast(fp32), ALU.subtract).then_inc(x_split, 1)
                for e in range(1, NE + 1):
                    split_weights(e)

            @block.scalar
            def _(act):
                act.wait_ge(exp_in, 1)
                nc.scalar.activation(lg[:], lg[:], ACT.Exp).then_inc(exp_done, 1)
                for e in range(NE):
                    with act.Fori(0, ROUNDS) as i:
                        for s in range(2):
                            _, nb, t0, t1, _, _ = JOBS[e][s]
                            for f in range(FC):
                                m = ((e * ROUNDS * 2 + s) * FC + f) // 2 + i * FC
                                gelu(act, ph, vec("eb1", e * FC + f, e * FC + f + 1), f, m, nb * (t1 - t0))

            @block.vector
            def _(dve):
                s = Steps(dve, dve_step)
                for c in range(DC):
                    nc.vector.tensor_copy(xhi[:, c], XT[:, c]).then_inc(x_hi, 1)
                for n, (a, z) in enumerate(SEG):
                    for c in range(DC):
                        s.op(nc.vector.reduce_sum(segs[:, n, c], XT[:, c, :, a:z], AX.X))
                s.fence()
                s.op(nc.vector.tensor_tensor(agg[:, 1], segs[:, 0], segs[:, 2], ALU.add))
                s.link(nc.vector.tensor_tensor(agg[:, 2], segs[:, 1], segs[:, 2], ALU.add))
                s.link(nc.vector.tensor_tensor(agg[:, 0], agg[:, 1], segs[:, 1], ALU.add))
                sizes = [z - a for a, z in SEG]
                for n, count in enumerate((T, sizes[0] + sizes[2], sizes[1] + sizes[2])):
                    s.op(nc.vector.tensor_scalar(agg[:, n], agg[:, n], 1.0 / count, None, ALU.mult))
                s.fence()
                s.op(nc.vector.tensor_tensor(prod[:], agg[:].rearrange("p n c b -> p (n c) b").unsqueeze(3).broadcast_to([P, 3 * DC, B, NE]),
                                             vec("gate_w").rearrange("p (k e) -> p k e", e=NE).unsqueeze(2).broadcast_to([P, 3 * DC, B, NE]),
                                             ALU.mult))
                nc.vector.tensor_tensor(prod2[:], silu[:].unsqueeze(3).broadcast_to([P, DC, B, 2 * NE]),
                                        vec("time_w").rearrange("p (k e) -> p k e", e=2 * NE).unsqueeze(2).broadcast_to([P, DC, B, 2 * NE]),
                                        ALU.mult).then_inc(gate_in, 1)
                dve.wait_ge(gate_mm, 1)
                s.op(nc.vector.tensor_tensor(lg[:], pgate[:].rearrange("p (b e) -> p b e", e=NE),
                                             vec("gate_b").unsqueeze(1).broadcast_to([P, B, NE]), ALU.add))
                s.link(nc.vector.tensor_tensor(md[:], ptime[:].rearrange("p (b e) -> p b e", e=2 * NE),
                                               vec("time_b").unsqueeze(1).broadcast_to([P, B, 2 * NE]), ALU.add))
                s.link(nc.vector.scalar_tensor_tensor(out=lg[:], in0=md[:, :, 0:NE], scalar=1.0, in1=lg[:], op0=ALU.add, op1=ALU.mult))
                s.link(nc.vector.tensor_tensor(lg[:], lg[:], md[:, :, NE:2 * NE], ALU.add))
                s.link(nc.vector.reduce_max(red[:], lg[:], AX.X))
                nc.vector.tensor_tensor(lg[:], lg[:], red[:].unsqueeze(2).broadcast_to([P, B, NE]), ALU.subtract).then_inc(exp_in, 1)
                dve.wait_ge(exp_done, 1)
                s.link(nc.vector.reduce_sum(red[:], lg[:], AX.X))
                s.link(nc.vector.reciprocal(red[:], red[:]))
                s.link(nc.vector.tensor_tensor(lg[:], lg[:], red[:].unsqueeze(2).broadcast_to([P, B, NE]), ALU.mult))
                mine = lg[:].unsqueeze(3).broadcast_to([P, B, NE, NE])
                other = lg[:].unsqueeze(2).broadcast_to([P, B, NE, NE])
                s.op(nc.vector.tensor_tensor(gt[:], other, mine, ALU.is_gt))
                s.link(nc.vector.tensor_tensor(eq[:], other, mine, ALU.is_equal))
                dve.wait_ge(tables, 5)
                s.link(nc.vector.tensor_tensor(eq[:], eq[:], earlier[:].unsqueeze(1).broadcast_to([P, B, NE, NE]), ALU.mult))
                s.link(nc.vector.tensor_tensor(gt[:], gt[:], eq[:], ALU.add))
                s.link(nc.vector.reduce_sum(we[:], gt[:], AX.X))
                s.link(nc.vector.tensor_scalar(we[:], we[:], 1.5, None, ALU.is_lt))
                s.link(nc.vector.tensor_tensor(we[:], we[:], lg[:], ALU.mult))
                s.link(nc.vector.reduce_sum(red[:], we[:], AX.X))
                s.link(nc.vector.tensor_scalar(red[:], red[:], 1e-8, None, ALU.add))
                s.link(nc.vector.reciprocal(red[:], red[:]))
                s.link(nc.vector.tensor_tensor(we[:], we[:], red[:].unsqueeze(2).broadcast_to([P, B, NE]), ALU.mult))
                for n in range(4):
                    for k, seen in enumerate(KEPT):
                        if n >= len(seen):
                            continue
                        e = seen[n]
                        for c in range(DC):
                            bias = vec("eb2", e * DC + c, e * DC + c + 1)
                            if n == 0:
                                s.op(nc.vector.tensor_scalar(bt[:, c, :, k], we[:, :, e], bias, vec("sb2", c, c + 1), ALU.mult, ALU.add))
                            else:
                                s.op(nc.vector.scalar_tensor_tensor(out=bt[:, c, :, k], in0=we[:, :, e], scalar=bias,
                                                                    in1=bt[:, c, :, k], op0=ALU.mult, op1=ALU.add))
                    s.fence()
                dve.wait_ge(x_split, DC)
                for c in range(DC):
                    for k, (a, z) in enumerate(SEG):
                        s.op(nc.vector.tensor_tensor(XT[:, c, :, a:z], XT[:, c, :, a:z],
                                                     bt[:, c, :, k:k + 1].broadcast_to([P, B, z - a]), ALU.add))
                s.fence()
                at = s.n
                for e in range(NE):
                    each = sum(job[1] for job in JOBS[e])
                    with dve.Fori(0, ROUNDS) as i:
                        done = 0
                        for s_ in range(2):
                            b0, nb, t0, t1, k0, k1 = JOBS[e][s_]
                            n = nb * (t1 - t0)
                            for f in range(FC):
                                m = ((e * ROUNDS * 2 + s_) * FC + f) // 2 + i * FC
                                split_hidden(dve, f, m, n)
                            dve.wait_ge(down_done[(FC - 1) % 2], m + 1)
                            for b in range(nb):
                                xv = XT[:, :, bass.ds(4 * i + (b0 + b), 1), k0:k1].rearrange("p c o t -> p c (o t)")
                                y0 = b * (t1 - t0) + k0 - t0
                                ins = nc.vector.scalar_tensor_tensor(
                                    out=xv, in0=py[s_][:, :, y0:y0 + k1 - k0],
                                    scalar=we[:].rearrange("p b e -> p e b")[:, e, bass.ds(4 * i + (b0 + b), 1)], in1=xv,
                                    op0=ALU.mult, op1=ALU.add)
                                ins.then_inc(y_free if b == nb - 1 else dve_step, 1)
                    dve.wait_ge(y_free, 2 * (e + 1) * ROUNDS)

            @block.tensor
            def _(pe):
                pe.wait_ge(gate_in, 1)
                pe.wait_ge(tables, 1)
                for k in range(3 * DC):
                    nc.tensor.matmul(pgate[:], ones[:], prod[:, k].rearrange("p b e -> p (b e)"), start=(k == 0), stop=(k == 3 * DC - 1))
                for k in range(DC):
                    i = nc.tensor.matmul(ptime[:], ones[:], prod2[:, k].rearrange("p b e -> p (b e)"), start=(k == 0), stop=(k == DC - 1))
                i.then_inc(gate_mm, 1)
                pe.wait_ge(x_split, DC)
                for e in range(NE):
                    pe.wait_ge(w_split, e + 1)
                    with pe.Fori(0, ROUNDS) as i:
                        for s in range(2):
                            b0, nb, t0, t1, _, _ = JOBS[e][s]
                            n, xs = nb * (t1 - t0), (slice(None), bass.ds(4 * i + b0, nb), slice(t0, t1))

                            def issue(ops, done):
                                for o in ops:
                                    ins = o()
                                ins.then_inc(done, 1)
                            for f in range(FC + 1):
                                if f < FC:
                                    m = ((e * ROUNDS * 2 + s) * FC + f) // 2 + i * FC
                                    pe.wait_ge(gelu_done[f % 2], m)
                                    issue(up(pe, ph, e % 2, f, xs, n), up_done[f % 2])
                                if f > 0:
                                    m = ((e * ROUNDS * 2 + s) * FC + f - 1) // 2 + i * FC
                                    pe.wait_ge(lo_done[(f - 1) % 2], m + 1)
                                    if f == 1:
                                        prior = 2 * (e * ROUNDS + i) + s - 1
                                        pe.wait_ge(y_free, prior if not (e == 0 and s == 0) else 2 * i)
                                    issue(down(pe, py[s], e % 2, f - 1, n), down_done[(f - 1) % 2])
                    pe.wait_ge(down_done[1], (e + 1) * ROUNDS * FC)
                    pe.sem_inc(w_used, 1)

        shared_and_rnn(nc, env, locals())


def shared_and_rnn(nc, env, ex):
    fp32, ALU, ACT = (env[k] for k in ("fp32", "ALU", "ACT"))
    sb, ps, sem, vec = (env[k] for k in ("sb", "ps", "sem", "vec"))
    XT, wx, wh, out = (env[k] for k in ("XT", "wx_sb", "wh_sb", "out"))
    up, down, gelu, split_hidden = (ex[k] for k in ("up", "down", "gelu", "split_hidden"))
    up_done, gelu_done, lo_done, down_done = (ex[k] for k in ("up_done", "gelu_done", "lo_done", "down_done"))
    N = B * CH
    BUF = NE % 2
    M0 = NE * 4 * FC
    st = ExitStack()
    with st:
        hs = sb(st, "hs", [P, 2, CH, DC, B])
        staged = sb(st, "staged", [P, 2, DC, B, CH])
        ones = sb(st, "ones_row", [1, N])
        ph = [ps(st, f"phs{q}", [P, 512]) for q in range(2)]
        py = ps(st, "pys", [P, DC, 512])
        pr = [ps(st, f"pr{q}", [P, DC, CH, B]) for q in range(2)]
        ones_set, half_added, x_ready, step_done, tanh_done = (
            sem(st, n) for n in ("ones_set", "half_added", "x_ready", "step_done", "tanh_done"))
        staged_done, out_done = ([sem(st, f"{n}{s}") for s in range(2)] for n in ("staged_done", "out_done"))
        block = st.enter_context(nc.Block())

        def chunk_loop(eng, chunk, recur, last):
            chunk(0, 0, None)
            with eng.Fori(0, NCH // 2 - 1) as i:
                chunk(2 * i + 1, 1, i)
                chunk(2 * i + 2, 0, i)
            chunk(NCH - 1, 1, NCH // 2 - 1)
            for k in range(CH):
                recur(NCH // 2 - 1, 1, k)
            last(NCH // 2 - 1, 1)

        def steps_by(f):
            return 0 if f < 0 else CH // FC // 2 if f == 0 else CH // FC * f if f < FC else CH

        @block.tensor
        def _(pe):
            def recur(q, s, k):
                pe.wait_ge(tanh_done, CH * (2 * q + s) + k)
                prev = hs[:, s, k - 1] if k > 0 else hs[:, 1 - s, CH - 1]
                for m in range(DC):
                    for c in range(DC):
                        i = nc.tensor.matmul(pr[s][:, m, k], wh[:, c, m * P:(m + 1) * P], prev[:, c],
                                             start=False, stop=(c == DC - 1), skip_group_check=True)
                i.then_inc(step_done, 1)

            def chunk(c, s, q):
                xs = (slice(None), slice(0, B), bass.ds(CH * c, CH))
                steps = list(range(CH))

                def spread(ops, done):
                    for n, o in enumerate(ops):
                        ins = o()
                        if n == len(ops) - 1:
                            ins.then_inc(done, 1)
                        if n % 3 == 2 and q is not None:
                            recur(q, 1 - s, steps.pop(0))
                for f in range(FC + 1):
                    if f < FC:
                        pe.wait_ge(gelu_done[f % 2], M0 + c * (FC // 2) + f // 2)
                        spread(up(pe, ph, BUF, f, xs, N), up_done[f % 2])
                    if f > 0:
                        pe.wait_ge(lo_done[(f - 1) % 2], M0 + c * (FC // 2) + (f - 1) // 2 + 1)
                        if f == 1:
                            pe.wait_ge(x_ready, c)
                        spread(down(pe, py, BUF, f - 1, N), down_done[(f - 1) % 2])
                assert q is None or not steps
                pe.wait_ge(x_ready, c + 1)
                for m in range(DC):
                    dst = pr[s][:, m].rearrange("p t b -> p (t b)")
                    nc.tensor.matmul(dst, vec("rnn_b_row")[0:1, m * P:(m + 1) * P], ones[:, :], start=True, stop=False)
                    for k in range(DC):
                        nc.tensor.matmul(dst, wx[:, k, m * P:(m + 1) * P],
                                         XT[:, k, :, bass.ds(CH * c, CH)].rearrange("p b t -> p t b"), start=False, stop=(k == DC - 1))
            pe.wait_ge(ones_set, 2)
            chunk_loop(pe, chunk, recur, lambda r, s: None)

        @block.scalar
        def _(act):
            def recur(q, s, k):
                act.wait_ge(step_done, CH * (2 * q + s) + k + 1)
                if k == 0:
                    act.wait_ge(staged_done[s], q)
                nc.scalar.activation(hs[:, s, k], pr[s][:, :, k], ACT.Tanh).then_inc(tanh_done, 1)

            def chunk(c, s, q):
                for f in range(FC + 1):
                    if q is not None:
                        for k in range(steps_by(f - 1), steps_by(f)):
                            recur(q, 1 - s, k)
                    if f < FC:
                        gelu(act, ph, vec("sb1", f, f + 1), f, M0 + c * (FC // 2) + f // 2, N)
            chunk_loop(act, chunk, recur, lambda r, s: None)

        @block.vector
        def _(dve):
            nc.vector.memset(ones[:, :], 1.0).then_inc(ones_set, 1)
            nc.vector.tensor_copy(hs[:, 1, CH - 1], vec("cond").rearrange("p (c b) -> p c b", c=DC)).then_inc(ones_set, 1)

            def stage(q, s):
                r = 2 * q + s
                dve.wait_ge(tanh_done, CH * (r + 1))
                dve.wait_ge(out_done[s], 16 * q)
                nc.vector.tensor_tensor(staged[:, s], XT[:, :, :, bass.ds(CH * r, CH)],
                                        hs[:, s].rearrange("p t c b -> p c b t"), ALU.add).then_inc(staged_done[s], 1)

            def chunk(c, s, q):
                for f in range(FC):
                    split_hidden(dve, f, M0 + c * (FC // 2) + f // 2, N)
                dve.wait_ge(down_done[(FC - 1) % 2], M0 + c * (FC // 2) + FC // 2)
                for m in range(DC):
                    xv = XT[:, m, :, bass.ds(CH * c, CH)]
                    i = nc.vector.tensor_tensor(xv, xv, py[:, m].rearrange("p (b t) -> p b t", b=B), ALU.add)
                    i.then_inc(half_added if m == 0 else x_ready, 1)
                if q is not None:
                    stage(q, 1 - s)
            chunk_loop(dve, chunk, lambda r, s, k: None, stage)

        @block.sync
        def _(sp):
            def send(q, s):
                c = 2 * q + s
                sp.wait_ge(staged_done[s], q + 1)
                sp.dma_start(out[bass.ds(c, 1)].rearrange("o p n -> p (o n)"), staged[:, s].rearrange("p c b t -> p (c b t)")).then_inc(out_done[s], 16)
            with sp.Fori(0, NCH // 2) as i:
                send(i, 0)
                send(i, 1)
            for s in range(2):
                sp.wait_ge(out_done[s], 16 * (NCH // 2))


_INS = ["x_tok", "x_dm", "small", "mod_w", "w_qkv", "w_out", "w_fih", "ew1", "ew2", "sw1", "sw2", "wx", "wh"]


def kernel(x, cond_1024, L0_cond_position, L0_cond_mod_w, L0_cond_mod_b, L0_cond_w_qkv, L0_cond_w_out,
           L0_cond_q_norm_w, L0_cond_k_norm_w, L1_cond_W_f, L1_cond_b_f, L1_cond_W_i, L1_cond_b_i, L1_cond_W_h,
           L1_cond_b_h, L2_cond_gate_w, L2_cond_gate_b, L2_cond_time_w, L2_cond_time_b, L2_cond_ew1, L2_cond_eb1,
           L2_cond_ew2, L2_cond_eb2, L2_cond_sw1, L2_cond_sb1, L2_cond_sw2, L2_cond_sb2, L3_cond_Wx, L3_cond_Wh,
           L3_cond_b):
    import numpy as np
    import concourse.bacc as bacc
    from concourse import mybir as mb
    from concourse.bass_utils import run_bass_kernel_spmd

    def columns(v):
        return np.reshape(np.asarray(v), (-1, P)).T

    def rows(w):
        w = np.asarray(w)
        return w.reshape(-1, P, w.shape[-1]).transpose(1, 0, 2).reshape(P, -1)

    def everywhere(*vs):
        v = np.concatenate([np.ravel(np.asarray(v)) for v in vs])
        return np.broadcast_to(v, (P, v.size))

    parts = {
        "mod_b": columns(L0_cond_mod_b), "b_f": columns(L1_cond_b_f), "b_i": columns(L1_cond_b_i),
        "b_h": columns(L1_cond_b_h), "eb1": columns(L2_cond_eb1), "sb1": columns(L2_cond_sb1),
        "eb2": columns(L2_cond_eb2), "sb2": columns(L2_cond_sb2), "rnn_b": columns(L3_cond_b),
        "cond": rows(np.asarray(cond_1024).T), "qk_w": everywhere(L0_cond_q_norm_w, L0_cond_k_norm_w),
        "gate_b": everywhere(L2_cond_gate_b), "time_b": everywhere(L2_cond_time_b), "gate_w": rows(L2_cond_gate_w),
        "time_w": rows(L2_cond_time_w), "pos": rows(np.asarray(L0_cond_position).reshape(T, ROT)), "rnn_b_row": everywhere(L3_cond_b),
    }
    xs = np.asarray(x)
    arrays = {
        "x_tok": xs, "x_dm": xs.transpose(2, 0, 1), "small": np.concatenate([parts[n] for n, _ in SMALL], axis=1),
        "mod_w": L0_cond_mod_w, "w_qkv": L0_cond_w_qkv, "w_out": L0_cond_w_out,
        "w_fih": np.concatenate([np.asarray(w).T for w in (L1_cond_W_f, L1_cond_W_i, L1_cond_W_h)], axis=1),
        "ew1": L2_cond_ew1, "ew2": L2_cond_ew2, "sw1": L2_cond_sw1, "sw2": L2_cond_sw2, "wx": L3_cond_Wx, "wh": L3_cond_Wh,
    }
    arrays = {n: np.ascontiguousarray(a) for n, a in arrays.items()}
    nc = bacc.Bacc("TRN2", target_bir_lowering=False, num_devices=1)
    args = [nc.dram_tensor("in_" + n, arrays[n].shape, mb.dt.from_np(arrays[n].dtype), kind="ExternalInput").ap() for n in _INS]
    out = nc.dram_tensor("out_dm", (NCH, P, DC * B * CH), mb.dt.float32, kind="ExternalOutput").ap()
    build(nc, *args, out)
    r = run_bass_kernel_spmd(nc, [{"in_" + n: a for n, a in arrays.items()}], core_ids=[0])
    o = np.asarray(r.results[0]["out_dm"]).reshape(NCH, P, DC, B, CH)
    return np.ascontiguousarray(o.transpose(3, 0, 4, 2, 1).reshape(B, T, D))
```

```python
import concourse.bass as bass
from concourse import mybir
from contextlib import ExitStack

P = 128
B, T, D = 16, 256, 256
DC = D // P
TC = T // P
HEADS, HD = 16, 16
HP = HEADS // 2
SLOT = 64
NE, F = 4, 1024
FC = F // P
ROT = HD // 2
SEG = [(0, T // 3), (T // 3, 2 * (T // 3)), (2 * (T // 3), T)]

SMALL = [("mod_b", 6), ("b_f", 2), ("b_i", 2), ("b_h", 2), ("eb1", NE * FC), ("sb1", FC), ("eb2", NE * DC),
         ("sb2", DC), ("rnn_b", DC), ("cond", DC * B), ("qk_w", 2 * HD), ("gate_b", NE), ("time_b", 2 * NE),
         ("gate_w", 3 * DC * NE), ("time_w", DC * 2 * NE), ("pos", TC * ROT), ("rnn_b_row", D)]
SMALL_AT, SMALL_W = {}, 0
for _name, _width in SMALL:
    SMALL_AT[_name] = SMALL_W
    SMALL_W += _width


def later(b):
    return not isinstance(b, int) or b > 0


PRIMED = 1


class Steps:

    def __init__(self, eng, sem, base=0):
        self.eng, self.sem, self.base, self.n, self.last = eng, sem, base, 0, None

    def op(self, ins, sem=None, value=None):
        if sem is None:
            self.n += 1
            sem, value = self.sem, self.base + self.n
        ins.then_inc(sem, 1)
        self.last = (sem, value)

    def fence(self):
        self.eng.wait_ge(*self.last)

    def link(self, ins, sem=None, value=None):
        self.op(ins, sem, value)
        self.fence()


def _round_fills():
    fills, taken = [], 0
    for h in range(HEADS):
        while taken < min(HEADS, (4 * h + 7) // 3):
            fills.append(("scores_max", taken, 1))
            taken += 1
        fills.append(("scores", h, 0))
        if h == 2:
            fills += [("norm_rows", 0, -1), ("norm_rows", 1, -1)]
        if h == 6:
            fills.append(("out_rows", 0, -1))
        if h == 9:
            fills.append(("project", 0, -1))
        if h == HEADS - 3:
            fills.append(("max_rows", 0, 1))
    return fills + [("qk_rows", j, 2) for j in range(8)]


FILLS = _round_fills()
PLACE = {f[:2]: n for n, f in enumerate(FILLS)}
ROT_BANKS = 3
WHOLE = 1


def bank_of(kind, j=0):
    return PLACE[kind, j] % ROT_BANKS


def fills_in(r, k, end=None):
    return sum(1 for n, f in enumerate(FILLS[:end]) if n % ROT_BANKS == k and 0 <= r + f[2] < B)


def fills_before_round(r, k):
    if isinstance(r, int):
        return sum(fills_in(q, k) for q in range(-2, r))
    return sum(fills_in(q, k) for q in range(-2, WHOLE)) - WHOLE * fills_in(WHOLE, k) + r * fills_in(WHOLE, k)


def fills_before(r, kind, j=0):
    n = PLACE[kind, j]
    return fills_before_round(r, n % ROT_BANKS) + fills_in(r if isinstance(r, int) else WHOLE, n % ROT_BANKS, n)


def build(nc, x_tok, x_dm, small_in, mod_w, w_qkv, w_out, w_fih, ew1, ew2, sw1, sw2, wx, wh, out):
    fp32, fp32r = mybir.dt.float32, mybir.dt.float32r
    ALU, ACT, AX = mybir.AluOpType, mybir.ActivationFunctionType, mybir.AxisListType
    hold = ExitStack()

    def sb(stack, name, shape, dt=fp32):
        return stack.enter_context(nc.sbuf_tensor(name, shape, dt))

    def ps(stack, name, shape):
        return stack.enter_context(nc.psum_tensor(name, shape, fp32))

    def sem(stack, name):
        return stack.enter_context(nc.semaphore(name))

    with hold:
        XT = sb(hold, "XT", [P, DC, B, T])
        small = sb(hold, "small", [P, SMALL_W])
        ident = sb(hold, "ident", [P, P])
        silu = sb(hold, "silu", [P, DC, B])
        eps8 = sb(hold, "eps8", [P, 1])
        wx_sb = sb(hold, "wx_sb", [P, DC, D])
        wh_sb = sb(hold, "wh_sb", [P, DC, D])
        later_loaded = sem(hold, "later_loaded")

        def vec(name, a=None, z=None):
            at = SMALL_AT[name]
            width = dict(SMALL)[name]
            return small[:, at + (a or 0):at + (width if z is None else z)]

        with ExitStack() as early:
            wfih_sb = sb(early, "wfih_sb", [P, DC, 3 * D])
            attention(nc, locals())
            recurrence(nc, locals())
        experts(nc, locals())


def attention(nc, env):
    fp32, fp32r, ALU, ACT, AX = (env[k] for k in ("fp32", "fp32r", "ALU", "ACT", "AX"))
    sb, ps, sem, vec = (env[k] for k in ("sb", "ps", "sem", "vec"))
    XT, small, ident, silu, eps8 = (env[k] for k in ("XT", "small", "ident", "silu", "eps8"))
    int32 = mybir.dt.int32
    st = ExitStack()
    with st:
        xn = sb(st, "xn", [P, B, TC, D])
        wqkv = sb(st, "wqkv", [P, DC, 3 * D])
        wout = sb(st, "wout", [P, DC, D])
        modw = sb(st, "modw", [P, DC, 3 * D])
        modT = sb(st, "modT", [P, 3 * DC, B])
        sig = sb(st, "sig", [P, DC, B])
        stats = sb(st, "stats", [P, B * TC, 6])
        mv = sb(st, "mv", [P, B * TC, 2])
        rstd = sb(st, "rstd", [P, B * TC])
        nmr = sb(st, "nmr", [P, B * TC])
        wmean = sb(st, "wmean", [P, DC, 2 * HEADS])
        ropeA = sb(st, "ropeA", [P, TC, 2, HD])
        ropeB = sb(st, "ropeB", [P, TC, 2, ROT // 2, 2])
        xh = sb(st, "xh", [P, TC, D])
        hT = sb(st, "hT", [P, DC, T])
        sq = sb(st, "sq", [P, TC * 2 * HEADS, HD])
        var = sb(st, "var", [P, TC * 2 * HEADS])
        newton = sb(st, "newton", [P, TC * 2 * HEADS])
        rs = sb(st, "rs", [P, TC * 2 * HEADS])
        y = sb(st, "y", [P, TC, 2, HEADS, HD])
        ya = sb(st, "ya", [P, TC, 2, HEADS, HD])
        yb = sb(st, "yb", [P, TC, 2, HEADS, ROT])
        slots = sb(st, "slots", [P, TC, 2, HEADS, SLOT], fp32r)
        QT = sb(st, "QT", [P, 2, HP, T], fp32r)
        KT = sb(st, "KT", [P, 2, HP, T], fp32r)
        vp = sb(st, "vp", [P, 2, TC, HEADS, 2 * HD])
        mx = sb(st, "mx", [P, TC, HEADS])
        nm = sb(st, "nm", [P, TC, HEADS], fp32r)
        mT = sb(st, "mT", [HEADS, T], fp32r)
        probs = sb(st, "probs", [P, 4, 2 * T])
        rden = sb(st, "rden", [P, TC, HEADS])
        oraw = sb(st, "oraw", [P, 2, 512])
        o = sb(st, "o", [P, TC, D])
        oT = sb(st, "oT", [P, DC, T])

        pA = ps(st, "pA", [P, 3, 512])
        pR = [ps(st, f"pR{k}", [P, 512]) for k in range(ROT_BANKS)]
        pO = ps(st, "pO", [P, 2, 512])

        small_in_s, w_in, modw_in, xT_in = (sem(st, n) for n in ("small_in_s", "w_in", "modw_in", "xT_in"))
        x_in = [sem(st, f"x_in{q}") for q in range(4)]
        pool_ready, sig_ready, mod_mm, silu_ready, dve_ready = (
            sem(st, n) for n in ("pool_ready", "sig_ready", "mod_mm", "silu_ready", "dve_ready"))
        dve_step, act_step, pool_step = (sem(st, n) for n in ("dve_step", "act_step", "pool_step"))
        xh_ready, x_rows, hT_ready, qkv_done, v_ready, sq_ready, sq_used, y_ready, ya_ready = (
            sem(st, n) for n in ("xh_ready", "x_rows", "hT_ready", "qkv_done", "v_ready", "sq_ready", "sq_used",
                                 "y_ready", "ya_ready"))
        slots_dve, slots_pool, hi_ready, nm_ready, max_moved, pv_done, oraw_ready, half_projected = (
            sem(st, n) for n in ("slots_dve", "slots_pool", "hi_ready", "nm_ready", "max_moved", "pv_done", "oraw_ready",
                                 "half_projected"))
        full = [sem(st, f"full{k}") for k in range(ROT_BANKS)]
        free = [sem(st, f"free{k}") for k in range(ROT_BANKS)]

        slots32 = slots[:].bitcast(fp32)
        qk_psum = pA[:, 1:3, :].rearrange("p t (g e) -> p (t g) e", e=HD)
        LOOP = (B - 3) // 2

        def rounds(eng, one):
            for r in range(-2, WHOLE):
                one(r, r % 2)
            with eng.Fori(0, LOOP) as i:
                one(2 * i + WHOLE, 1)
                one(2 * i + WHOLE + 1, 0)
            for r in range(WHOLE + 2 * LOOP, B + 1):
                one(r, r % 2)

        def has(r, ahead):
            return not isinstance(r, int) or 0 <= r + ahead < B

        def await_full(eng, r, kind, j=0):
            eng.wait_ge(full[bank_of(kind, j)], fills_before(r, kind, j) + 1)

        def await_read(eng, r, kind, j=0):
            eng.wait_ge(free[bank_of(kind, j)], fills_before(r, kind, j) + 1)

        def last_of(kind, count):
            return [max(j for j in range(count) if bank_of(kind, j) == k) for k in range(ROT_BANKS)]

        def evacuate_qk(eng, copy, r, par, j):
            dst = (QT, KT)[j // 4]
            g = j % 4
            await_full(eng, r, "qk_rows", j)
            k = bank_of("qk_rows", j)
            copy(dst[:, par, 2 * g:2 * g + 2], pR[k][:].rearrange("p (h t) -> p h t", h=2)).then_inc(free[k], 1)

        block = st.enter_context(nc.Block())

        @block.sync
        def _(sp):
            x_view = env["x_tok"].rearrange("b (c p) d -> p b c d", p=P)
            sp.dma_start(small[:, :], env["small_in"]).then_inc(small_in_s, 16)
            sp.dma_start(xn[:, 0:4], x_view[:, 0:4]).then_inc(x_in[0], 16)
            sp.dma_start(modw[:], env["mod_w"].rearrange("(c p) n -> p c n", p=P)).then_inc(modw_in, 16)
            sp.dma_start(wqkv[:], env["w_qkv"].rearrange("(c p) n -> p c n", p=P)).then_inc(w_in, 16)
            for q in range(1, 4):
                sp.dma_start(xn[:, 4 * q:4 * q + 4], x_view[:, 4 * q:4 * q + 4]).then_inc(x_in[q], 16)
            sp.dma_start(wout[:], env["w_out"].rearrange("(c p) n -> p c n", p=P)).then_inc(xT_in, 16)
            for c in range(DC):
                sp.dma_start(XT[:, c], env["x_dm"][c * P:(c + 1) * P]).then_inc(xT_in, 16)
            later = env["later_loaded"]
            sp.dma_start(env["wfih_sb"][:], env["w_fih"].rearrange("(c p) n -> p c n", p=P)).then_inc(later, 16)
            sp.dma_start(env["wx_sb"][:], env["wx"].rearrange("(c p) n -> p c n", p=P)).then_inc(later, 16)
            sp.dma_start(env["wh_sb"][:], env["wh"].rearrange("(c p) n -> p c n", p=P)).then_inc(later, 16)

            def one(r, par):
                if has(r, 1):
                    await_read(sp, r, "max_rows")
                    for s in range(2):
                        row = SLOT * s + 3 * HD
                        sp.dma_start(QT[row:row + 1, 1 - par].bitcast(fp32), mT[s * HP:(s + 1) * HP, :].bitcast(fp32))\
                            .then_inc(max_moved, 16)
            rounds(sp, one)
            sp.wait_ge(max_moved, 32 * B)

        @block.gpsimd
        def _(pool):
            s = Steps(pool, pool_step)
            s.link(nc.gpsimd.memset(ident[:], 0.0))
            s.op(nc.gpsimd.affine_select(out=ident[:], in_=ident[:], compare_op=ALU.not_equal, fill=1.0, base=0,
                                         pattern=[[-1, P]], channel_multiplier=1))
            s.op(nc.gpsimd.memset(vp[:], 1.0))
            s.op(nc.gpsimd.memset(eps8[:], 1e-8))
            s.link(nc.gpsimd.memset(slots32, 0.0))
            nc.gpsimd.memset(slots32[:, :, 1, :, 3 * HD:3 * HD + 1], 1.0).then_inc(pool_ready, 1)
            pool.wait_ge(pool_ready, 1)

            def one(r, par):
                if not has(r, 2):
                    return
                b = r + 2
                s = Steps(pool, pool_step, 5 + 4 * b)
                pool.wait_ge(y_ready, b + 1)
                if later(b):
                    pool.wait_ge(slots_dve, b)
                for q in range(2):
                    s.op(nc.gpsimd.tensor_tensor(
                        yb[:, :, :, :, q::2].rearrange("p t q h j -> p (t q) h j"),
                        y[:, :, :, :, 1 - q:ROT:2].rearrange("p t q h j -> p (t q) h j"),
                        ropeB[:, :, :, :, q].rearrange("p t q j -> p (t q) j").unsqueeze(2)
                        .broadcast_to([P, 2 * TC, HEADS, ROT // 2]), ALU.mult))
                s.link(nc.gpsimd.tensor_tensor(
                    ya[:].rearrange("p t q h e -> p (t q) h e"), y[:].rearrange("p t q h e -> p (t q) h e"),
                    ropeA[:].rearrange("p t q e -> p (t q) e").unsqueeze(2).broadcast_to([P, 2 * TC, HEADS, HD]), ALU.mult))
                yav = ya[:, :, :, :, 0:ROT].rearrange("p t q h j -> p (t q) h j")
                nc.gpsimd.tensor_tensor(yav, yav, yb[:].rearrange("p t q h j -> p (t q) h j"), ALU.add).then_inc(ya_ready, 1)
                pool.wait_ge(hi_ready, b + 1)
                s.op(nc.gpsimd.tensor_tensor(slots[:, :, 0, :, HD:2 * HD], ya[:, :, 0], slots32[:, :, 0, :, 0:HD], ALU.subtract))
                s.op(nc.gpsimd.tensor_tensor(slots[:, :, 1, :, 2 * HD:3 * HD], ya[:, :, 1], slots32[:, :, 1, :, 0:HD], ALU.subtract),
                     slots_pool, b + 1)
                assert s.n == 4, s.n
            rounds(pool, one)

        @block.scalar
        def _(act):
            act.wait_ge(small_in_s, 16)
            nc.scalar.activation(sig[:].rearrange("p c b -> p (c b)"), vec("cond"), ACT.Sigmoid).then_inc(sig_ready, 1)

            def modulate(b):
                act.wait_ge(x_rows, b + 1)
                if later(b):
                    act.wait_ge(qkv_done, 2 * b)
                else:
                    act.wait_ge(dve_ready, 1)
                s = Steps(act, act_step, b)
                for c in range(DC):
                    i = nc.scalar.activation(hT[:, c], pA[:, 0, c * T:(c + 1) * T], ACT.Identity,
                                             bias=modT[:, c, bass.ds(b, 1)], scale=modT[:, DC + c, bass.ds(b, 1)])
                    s.op(i) if c == 0 else s.op(i, hT_ready, b + 1)

            def squares(b):
                act.wait_ge(qkv_done, 2 * (b + 1))
                if later(b):
                    act.wait_ge(sq_used, b)
                nc.scalar.activation(sq[:], qk_psum, ACT.Square).then_inc(sq_ready, 1)

            def copy_v(b, par):
                act.wait_ge(qkv_done, 2 * (b + 1))
                if not later(b):
                    act.wait_ge(pool_ready, 1)
                nc.scalar.activation(vp[:, par, :, :, 0:HD], pA[:, 0, :].rearrange("p (c h e) -> p c h e", c=TC, e=HD),
                                     ACT.Copy).then_inc(v_ready, 1)

            def one(r, par):
                for kind, j, ahead in FILLS:
                    if (kind, j) == ("scores", 1) and has(r, 2):
                        modulate(r + 2)
                    if (kind, j) == ("scores", 5) and has(r, 2):
                        squares(r + 2)
                    if (kind, j) == ("qk_rows", 0):
                        if has(r, 0):
                            act.wait_ge(pv_done, HEADS * (r + 1))
                            nc.scalar.copy(oraw[:], pO[:]).then_inc(oraw_ready, 1)
                        if has(r, 2):
                            copy_v(r + 2, par)
                    if not has(r, ahead):
                        continue
                    k = bank_of(kind, j)
                    if kind == "scores":
                        await_full(act, r, kind, j)
                        if j > 3 or later(r):
                            act.wait_ge(pv_done, HEADS * r + max(j - 3, 0))
                        nc.scalar.activation(probs[:, j % 4], pR[k][:], ACT.Exp, scale=HD ** -0.5).then_inc(free[k], 1)
                    elif kind == "max_rows":
                        await_full(act, r, kind, j)
                        if later(r + 1):
                            act.wait_ge(max_moved, 32 * (r + 1))
                        nc.scalar.copy(mT[:, :], pR[k][0:HEADS, 0:T]).then_inc(free[k], 1)
                    elif kind == "out_rows":
                        await_full(act, r, kind, j)
                        nc.scalar.copy(oT[:].rearrange("p c t -> p (c t)"), pR[k][:]).then_inc(free[k], 1)
                    elif kind == "qk_rows" and j % 2 == 0:
                        evacuate_qk(act, nc.scalar.copy, r, par, j)
            rounds(act, one)

        @block.vector
        def _(dve):
            s = Steps(dve, dve_step)

            def inverse_root(dst, v, tmp):
                s.link(nc.vector.tensor_scalar(dst.bitcast(int32), v.bitcast(int32), -0.5, float(0x5f3759df), ALU.mult, ALU.add))
                s.link(nc.vector.tensor_scalar(v, v, -0.5, None, ALU.mult))
                yield
                for _ in range(3):
                    s.link(nc.vector.tensor_tensor(tmp, dst, dst, ALU.mult))
                    s.link(nc.vector.tensor_tensor(tmp, tmp, v, ALU.mult))
                    yield
                    s.link(nc.vector.scalar_tensor_tensor(out=dst, in0=tmp, scalar=1.5, in1=dst, op0=ALU.add, op1=ALU.mult))

            def token_norms(a, z):
                n0, n1 = a * TC, z * TC
                for n in range(n0, n1):
                    s.op(nc.vector.bn_stats(stats[:, n], xn[:, n // TC, n % TC]))
                s.fence()
                for n in range(n0, n1):
                    s.op(nc.vector.bn_aggr(mv[:, n], stats[:, n]))
                s.fence()
                v = mv[:, n0:n1, 1]
                s.link(nc.vector.tensor_scalar(v, v, 1e-6, None, ALU.add))
                for _ in inverse_root(rstd[:, n0:n1], v, nmr[:, n0:n1]):
                    pass
                s.link(nc.vector.scalar_tensor_tensor(out=nmr[:, n0:n1], in0=mv[:, n0:n1, 0], scalar=-1.0, in1=rstd[:, n0:n1],
                                                      op0=ALU.mult, op1=ALU.mult))

            dve.wait_ge(small_in_s, 16)
            dve.wait_ge(sig_ready, 1)
            nc.vector.tensor_tensor(silu[:].rearrange("p c b -> p (c b)"), sig[:].rearrange("p c b -> p (c b)"),
                                    vec("cond"), ALU.mult).then_inc(silu_ready, 1)
            dve.wait_ge(x_in[0], 16)
            token_norms(0, 4)

            def normalise(b):
                if later(b):
                    dve.wait_ge(x_rows, b)
                for t in range(TC):
                    n = TC * b + t
                    nc.vector.tensor_scalar(xh[:, t], xn[:, bass.ds(b, 1), t].rearrange("p o d -> p (o d)"),
                                            rstd[:, bass.ds(n, 1)], nmr[:, bass.ds(n, 1)], ALU.mult, ALU.add).then_inc(xh_ready, 1)
            dve.wait_ge(mod_mm, 1)
            s.link(nc.vector.tensor_tensor(modT[:], pA[:, 1, 0:3 * DC * B].rearrange("p (m b) -> p m b", b=B),
                                           vec("mod_b").unsqueeze(2).broadcast_to([P, 3 * DC, B]), ALU.add))
            s.link(nc.vector.tensor_scalar(modT[:, DC:2 * DC], modT[:, DC:2 * DC], 1.0, None, ALU.add), dve_ready, 1)
            dve.wait_ge(w_in, 16)
            qk_w = wqkv[:, :, 0:2 * D].rearrange("p c (g e) -> p c g e", e=HD)
            s.link(nc.vector.reduce_sum(wmean[:], qk_w, AX.X))
            s.link(nc.vector.tensor_scalar(wmean[:], wmean[:], -1.0 / HD, None, ALU.mult))
            s.link(nc.vector.tensor_tensor(qk_w, qk_w, wmean[:].unsqueeze(3).broadcast_to([P, DC, 2 * HEADS, HD]), ALU.add), dve_ready, 2)
            w2 = vec("qk_w").rearrange("p (q e) -> p q e", q=2)
            pos = vec("pos").rearrange("p (t j i) -> p t j i", t=TC, i=2)
            wr = w2[:, :, 0:ROT].rearrange("p q (j i) -> p q j i", i=2)
            for t in range(TC):
                cos = pos[:, t, :, 0].unsqueeze(1).unsqueeze(3).broadcast_to([P, 2, ROT // 2, 2])
                sin = pos[:, t, :, 1].unsqueeze(1).broadcast_to([P, 2, ROT // 2])
                s.op(nc.vector.tensor_tensor(ropeA[:, t, :, 0:ROT].rearrange("p q (j i) -> p q j i", i=2), wr, cos, ALU.mult))
                s.op(nc.vector.tensor_copy(ropeA[:, t, :, ROT:HD], w2[:, :, ROT:HD]))
                s.op(nc.vector.scalar_tensor_tensor(out=ropeB[:, t, :, :, 0], in0=wr[:, :, :, 1], scalar=-1.0, in1=sin,
                                                    op0=ALU.mult, op1=ALU.mult))
                s.op(nc.vector.tensor_tensor(ropeB[:, t, :, :, 1], wr[:, :, :, 0], sin, ALU.mult))
            s.fence()
            PREP, OUT = 13, 2
            norms_at = s.n
            NORMS = 2 * 4 * TC + 1 + 11 + 1

            def one(r, par):
                nonlocal s
                if isinstance(r, int):
                    done = norms_at + PREP * min(r + 2, B) + OUT * max(r - 1, 0) + (3 * NORMS if r > -1 else 0)
                else:
                    done = norms_at + PREP * (r + 2) + OUT * (r - 1) + 3 * NORMS
                if has(r, 2):
                    normalise(r + 2)
                    root = root_of_squares(r + 2, done + (OUT if has(r, -1) else 0))
                    if not has(r, 1):
                        for _ in root:
                            pass
                for kind, j, ahead in FILLS:
                    if (kind, j) == ("qk_rows", 0) and has(r, 2):
                        high_parts(r + 2)
                    if not has(r, ahead):
                        continue
                    k = bank_of(kind, j)
                    if kind == "scores_max":
                        await_full(dve, r, kind, j)
                        nc.vector.reduce_max(mx[:, :, j], pR[k][:].rearrange("p (c k) -> p c k", c=TC), AX.X).then_inc(free[k], 1)
                        if has(r, 2) and j >= 8:
                            next(root, None)
                    elif kind == "max_rows":
                        for h in last_of("scores_max", HEADS):
                            await_read(dve, r, "scores_max", h)
                        nc.vector.tensor_scalar(nm[:].rearrange("p c (s g) -> p c g s", s=2),
                                                mx[:].rearrange("p c (g s) -> p c g s", s=2), -1.0, None, ALU.mult).then_inc(nm_ready, 1)
                    elif kind == "norm_rows":
                        if j == 0:
                            s = Steps(dve, dve_step, done)
                        await_full(dve, r, kind, j)
                        heads = pR[k][:].rearrange("p (h e) -> p h e", e=2 * HD)
                        s.link(nc.vector.reciprocal(rden[:, j], heads[:, :, HD]))
                        assert s.n == j + 1, s.n
                        nc.vector.tensor_tensor(o[:, j].rearrange("p (h e) -> p h e", e=HD), heads[:, :, 0:HD],
                                                rden[:, j].unsqueeze(2).broadcast_to([P, HEADS, HD]), ALU.mult).then_inc(free[k], 1)
                    elif kind == "project":
                        await_full(dve, r, kind, j)
                        dve.wait_ge(xT_in, 48)
                        for c in range(DC):
                            xv = XT[:, c, bass.ds(r - 1, 1)].rearrange("p o t -> p (o t)")
                            i = nc.vector.scalar_tensor_tensor(out=xv, in0=pR[k][:, c * T:(c + 1) * T],
                                                               scalar=modT[:, 2 * DC + c, bass.ds(r - 1, 1)], in1=xv,
                                                               op0=ALU.mult, op1=ALU.add)
                            i.then_inc(half_projected if c == 0 else free[k], 1)
                    elif kind == "qk_rows" and j % 2:
                        evacuate_qk(dve, nc.vector.tensor_copy, r, par, j)
                if isinstance(r, int) and r == -1:
                    s = Steps(dve, dve_step, norms_at + PREP * 2)
                    for q in range(1, 4):
                        dve.wait_ge(x_in[q], 16)
                        token_norms(4 * q, 4 * q + 4)
                    assert s.n == 3 * NORMS, (s.n, NORMS)

            def root_of_squares(b, done):
                nonlocal s
                s = Steps(dve, dve_step, done)
                dve.wait_ge(sq_ready, b + 1)
                s.link(nc.vector.reduce_sum(var[:], sq[:], AX.X), sq_used, b + 1)
                s.link(nc.vector.tensor_scalar(var[:], var[:], 1.0 / HD, 1e-6, ALU.mult, ALU.add))
                yield from inverse_root(rs[:], var[:], newton[:])
                yield
                if later(b):
                    dve.wait_ge(slots_pool, b)
                nc.vector.tensor_tensor(y[:].rearrange("p t q h e -> p (t q h) e"), qk_psum,
                                        rs[:].unsqueeze(2).broadcast_to([P, TC * 2 * HEADS, HD]), ALU.mult).then_inc(y_ready, 1)

            def high_parts(b):
                dve.wait_ge(ya_ready, b + 1)
                if later(b):
                    dve.wait_ge(x_rows, b + 1)
                else:
                    dve.wait_ge(pool_ready, 1)
                nc.vector.tensor_copy(slots[:, :, :, :, 0:HD].rearrange("p t q h e -> p (t q) h e"),
                                      ya[:].rearrange("p t q h e -> p (t q) h e")).then_inc(hi_ready, 1)
                s.op(nc.vector.tensor_copy(slots[:, :, 0, :, 2 * HD:3 * HD], ya[:, :, 0]))
                s.op(nc.vector.tensor_copy(slots[:, :, 1, :, HD:2 * HD], ya[:, :, 1]), slots_dve, b + 1)
                assert s.n == PREP, s.n
            rounds(dve, one)

        @block.tensor
        def _(pe):
            pe.wait_ge(silu_ready, 1)
            pe.wait_ge(modw_in, 16)
            for m in range(3 * DC):
                for c in range(DC):
                    i = nc.tensor.matmul(pA[:, 1, m * B:(m + 1) * B], modw[:, c, m * P:(m + 1) * P], silu[:, c],
                                         start=(c == 0), stop=(c == DC - 1))
            i.then_inc(mod_mm, 1)

            def filling(r, kind, j=0):
                k = bank_of(kind, j)
                if not isinstance(r, int) or fills_before(r, kind, j) > 0:
                    pe.wait_ge(free[k], fills_before(r, kind, j))
                return pR[k], full[k]

            def rows_of_x(b):
                pe.wait_ge(xh_ready, TC * (b + 1))
                if not later(b):
                    pe.wait_ge(pool_ready, 1)
                if later(b):
                    pe.wait_ge(v_ready, b)
                for c in range(DC):
                    for t in range(TC):
                        i = nc.tensor.transpose(pA[:, 0, c * T + t * P:c * T + (t + 1) * P], xh[:, t, c * P:(c + 1) * P], ident[:])
                i.then_inc(x_rows, 1)

            def qkv(b, t):
                pe.wait_ge(hT_ready, b + 1)
                if later(b):
                    pe.wait_ge(y_ready, b)
                else:
                    pe.wait_ge(dve_ready, 2)
                for dst, a, z in ((pA[:, 1 + t, :], 0, 2 * D), (pA[:, 0, t * D:(t + 1) * D], 2 * D, 3 * D)):
                    for c in range(DC):
                        i = nc.tensor.matmul(dst, hT[:, c, t * P:(t + 1) * P], wqkv[:, c, a:z], start=(c == 0), stop=(c == DC - 1))
                i.then_inc(qkv_done, 1)

            def rows_of_qk(r, j):
                bank, done = filling(r, "qk_rows", j)
                for g in range(2):
                    for t in range(TC):
                        h = 2 * (2 * (j % 4) + g)
                        i = nc.tensor.transpose(bank[:, g * T + t * P:g * T + (t + 1) * P],
                                                slots32[:, t, j // 4, h:h + 2].rearrange("p h e -> p (h e)"), ident[:])
                i.then_inc(done, 1)

            def one(r, par):
                def scores_max(h):
                    lo, g = SLOT * (h % 2), h // 2
                    bank, done = filling(r, "scores_max", h)
                    for t in range(TC):
                        i = nc.tensor.matmul(bank[:, t * T:(t + 1) * T], QT[lo:lo + 3 * HD, 1 - par, g, t * P:(t + 1) * P],
                                             KT[lo:lo + 3 * HD, 1 - par, g], start=True, stop=True)
                    i.then_inc(done, 1)

                def scores(h):
                    lo, g = SLOT * (h % 2), h // 2
                    bank, done = filling(r, "scores", h)
                    for c in range(TC):
                        i = nc.tensor.matmul(bank[:, c * T:(c + 1) * T], KT[lo:lo + 3 * HD + 1, par, g, c * P:(c + 1) * P],
                                             QT[lo:lo + 3 * HD + 1, par, g], start=True, stop=True)
                    i.then_inc(done, 1)

                def values(h):
                    await_read(pe, r, "scores", h)
                    lo, g = 2 * HD * (h % 4), h // 4
                    for c in range(TC):
                        i = nc.tensor.matmul(pO[lo:lo + 2 * HD, g // 2, T * (g % 2):T * (g % 2) + T], vp[:, par, c, h],
                                             probs[:, h % 4, c * T:(c + 1) * T], start=(c == 0), stop=(c == TC - 1))
                    i.then_inc(pv_done, 1)

                if has(r, 1):
                    for k in range(ROT_BANKS):
                        pe.wait_ge(free[k], fills_before_round(r, k))
                if has(r, 0):
                    pe.wait_ge(max_moved, 32 * (r + 1))
                    if later(r):
                        pe.wait_ge(oraw_ready, r)
                    pe.wait_ge(v_ready, r + 1)
                if has(r, 2) and not has(r, 1):
                    rows_of_x(r + 2)
                    qkv(r + 2, 0)
                    qkv(r + 2, 1)
                for kind, j, ahead in FILLS:
                    if kind == "scores" and has(r, 1) and has(r, 2):
                        if j == 0:
                            rows_of_x(r + 2)
                        if j in (2, 3):
                            qkv(r + 2, j - 2)
                    if not has(r, ahead):
                        continue
                    if kind == "scores_max":
                        scores_max(j)
                    elif kind == "scores":
                        scores(j)
                        if j >= 2:
                            values(j - 2)
                        if j == HEADS - 1:
                            values(HEADS - 2)
                            values(HEADS - 1)
                    elif kind == "max_rows":
                        bank, done = filling(r, kind)
                        pe.wait_ge(nm_ready, r + 2)
                        for t in range(TC):
                            i = nc.tensor.transpose(bank[0:HEADS, t * P:(t + 1) * P], nm[:, t].bitcast(fp32), ident[:])
                        i.then_inc(done, 1)
                    elif kind == "qk_rows":
                        if j == 0:
                            pe.wait_ge(slots_dve, r + 3)
                            pe.wait_ge(slots_pool, r + 3)
                        rows_of_qk(r, j)
                    elif kind == "norm_rows":
                        bank, done = filling(r, kind, j)
                        pe.wait_ge(oraw_ready, r)
                        for g in range(4):
                            i = nc.tensor.transpose(bank[:, g * P:(g + 1) * P],
                                                    oraw[:, g // 2, T * (g % 2) + j * P:T * (g % 2) + (j + 1) * P], ident[:])
                        i.then_inc(done, 1)
                    elif kind == "out_rows":
                        bank, done = filling(r, kind)
                        for t in range(TC):
                            await_read(pe, r, "norm_rows", t)
                        for c in range(DC):
                            for t in range(TC):
                                i = nc.tensor.transpose(bank[:, c * T + t * P:c * T + (t + 1) * P],
                                                        o[:, t, c * P:(c + 1) * P], ident[:])
                        i.then_inc(done, 1)
                    else:
                        bank, done = filling(r, "project")
                        await_read(pe, r, "out_rows")
                        pe.wait_ge(xT_in, 48)
                        for m in range(DC):
                            for c in range(DC):
                                i = nc.tensor.matmul(bank[:, m * T:(m + 1) * T], wout[:, c, m * P:(m + 1) * P], oT[:, c],
                                                     start=(c == 0), stop=(c == DC - 1))
                        i.then_inc(done, 1)
            rounds(pe, one)


def recurrence(nc, env):
    fp32, ALU, ACT = (env[k] for k in ("fp32", "ALU", "ACT"))
    sb, ps, sem, vec = (env[k] for k in ("sb", "ps", "sem", "vec"))
    XT, eps8, wfih = (env[k] for k in ("XT", "eps8", "wfih_sb"))
    N = 2 * T
    st = ExitStack()
    with st:
        zeros = sb(st, "zeros", [P, T])
        fg = sb(st, "fg", [P, 2, N])
        ig = sb(st, "ig", [P, 2, N])
        total = sb(st, "total", [P, 2, N])
        inv = sb(st, "inv", [P, 2, N])
        new = sb(st, "new", [P, 2, N])
        logs = sb(st, "logs", [P, 2, 2, T + 1])
        scaling = sb(st, "scaling", [P, 2, N])
        decay = sb(st, "decay", [P, 2, N])
        hid = sb(st, "hid", [P, 2, N])
        pg = [ps(st, f"pg{u}", [P, 3, N]) for u in range(2)]
        dve_step, pool_step, act_step = (sem(st, n) for n in ("dve_step2", "pool_step2", "act_step2"))
        zeros_ready = sem(st, "zeros_ready")
        products, gates, summed, inverse, normed, log_ready, cum, scales, hid_ready, added, mult_done, run_done = (
            [sem(st, f"{n}{u}") for u in range(2)] for n in
            ("products", "gates", "summed", "inverse", "normed", "log_ready", "cum", "scales", "hid_ready", "added",
             "mult_done", "run_done"))
        block = st.enter_context(nc.Block())
        PAIRS = B // 2


        @block.sync
        def _(sp):
            for pair in (gates, cum, normed, log_ready, hid_ready, scales, added):
                for signal in pair:
                    sp.sem_inc(signal, PRIMED)

        @block.tensor
        def _(pe):
            pe.wait_ge(env["later_loaded"], 48)

            def unit(p, u):
                pe.wait_ge(gates[u], PRIMED + 2 * p)
                pe.wait_ge(cum[u], PRIMED + 2 * p)
                for g in range(3):
                    for c in range(DC):
                        i = nc.tensor.matmul(pg[u][:, g], wfih[:, c, g * D + u * P:g * D + (u + 1) * P],
                                             XT[:, c, bass.ds(2 * p, 2)], start=(c == 0), stop=(c == DC - 1))
                i.then_inc(products[u], 1)
            with pe.Fori(0, PAIRS) as p:
                unit(p, 0)
                unit(p, 1)

        def flow(eng, first, second, third):
            first(0, 0)
            with eng.Fori(0, PAIRS - 1) as p:
                second(p, 0)
                first(p, 1)
                third(p, 0)
                second(p, 1)
                first(p + 1, 0)
                third(p, 1)
            second(PAIRS - 1, 0)
            first(PAIRS - 1, 1)
            third(PAIRS - 1, 0)
            second(PAIRS - 1, 1)
            third(PAIRS - 1, 1)

        @block.scalar
        def _(act):
            def first(p, u):
                act.wait_ge(products[u], p + 1)
                act.wait_ge(normed[u], PRIMED + 2 * p)
                act.wait_ge(log_ready[u], PRIMED + p)
                nc.scalar.activation(fg[:, u], pg[u][:, 0], ACT.Sigmoid, bias=vec("b_f", u, u + 1)).then_inc(gates[u], 1)
                nc.scalar.activation(ig[:, u], pg[u][:, 1], ACT.Sigmoid, bias=vec("b_i", u, u + 1)).then_inc(gates[u], 1)

            def second(p, u):
                act.wait_ge(normed[u], PRIMED + 2 * p + 1)
                nc.scalar.activation(fg[:, u], fg[:, u], ACT.Ln, bias=eps8[:, 0:1]).then_inc(log_ready[u], 1)

            def third(p, u):
                act.wait_ge(cum[u], PRIMED + 2 * p + 2)
                act.wait_ge(hid_ready[u], PRIMED + p)
                for j in range(2):
                    nc.scalar.activation(scaling[:, u, j * T:(j + 1) * T], logs[:, u, j, 0:T], ACT.Exp,
                                         bias=logs[:, u, j, T:T + 1], scale=-1.0).then_inc(act_step, 1)
                nc.scalar.activation(decay[:, u].rearrange("p (j t) -> p j t", j=2), logs[:, u, :, 1:T + 1], ACT.Exp).then_inc(scales[u], 1)
            flow(act, first, second, third)

        @block.gpsimd
        def _(pool):
            def first(p, u):
                pool.wait_ge(gates[u], PRIMED + 2 * p + 2)
                s = Steps(pool, pool_step, 2 * p + u)
                s.link(nc.gpsimd.tensor_tensor(total[:, u], fg[:, u], ig[:, u], ALU.add))
                nc.gpsimd.tensor_tensor(total[:, u], total[:, u], eps8[:, 0:1].broadcast_to([P, N]), ALU.add).then_inc(summed[u], 1)

            def second(p, u):
                pool.wait_ge(inverse[u], p + 1)
                nc.gpsimd.tensor_tensor(fg[:, u], fg[:, u], inv[:, u], ALU.mult).then_inc(normed[u], 1)
                nc.gpsimd.tensor_tensor(ig[:, u], ig[:, u], inv[:, u], ALU.mult).then_inc(normed[u], 1)

            def third(p, u):
                pool.wait_ge(hid_ready[u], PRIMED + p + 1)
                pool.wait_ge(products[1], p + 1)
                xv = XT[:, u, bass.ds(2 * p, 2)]
                nc.gpsimd.tensor_tensor(xv, xv, hid[:, u].rearrange("p (j t) -> p j t", j=2), ALU.add).then_inc(added[u], 1)
            flow(pool, first, second, third)

        @block.vector
        def _(dve):
            nc.vector.memset(logs[:, :, :, 0:1], 0.0).then_inc(zeros_ready, 1)
            nc.vector.memset(zeros[:], 0.0).then_inc(zeros_ready, 1)
            dve.wait_ge(zeros_ready, 2)

            def first(p, u):
                dve.wait_ge(summed[u], p + 1)
                dve.wait_ge(normed[u], PRIMED + 2 * p)
                nc.vector.reciprocal(inv[:, u], total[:, u]).then_inc(inverse[u], 1)

            def second(p, u):
                dve.wait_ge(log_ready[u], PRIMED + p + 1)
                dve.wait_ge(normed[u], PRIMED + 2 * p + 2)
                dve.wait_ge(scales[u], PRIMED + p)
                nc.vector.scalar_tensor_tensor(out=new[:, u], in0=pg[u][:, 2], scalar=vec("b_h", u, u + 1), in1=ig[:, u],
                                               op0=ALU.add, op1=ALU.mult).then_inc(dve_step, 1)
                for j in range(2):
                    nc.vector.tensor_tensor_scan(logs[:, u, j, 1:T + 1], fg[:, u, j * T:(j + 1) * T], zeros[:], 0.0,
                                                 ALU.add, ALU.add).then_inc(cum[u], 1)

            def third(p, u):
                dve.wait_ge(scales[u], PRIMED + p + 1)
                dve.wait_ge(added[u], PRIMED + p)
                i = nc.vector.tensor_tensor(new[:, u], scaling[:, u], new[:, u], ALU.mult)
                i.then_inc(mult_done[u], 1)
                dve.wait_ge(mult_done[u], p + 1)
                for j in range(2):
                    nc.vector.tensor_tensor_scan(hid[:, u, j * T:(j + 1) * T], new[:, u, j * T:(j + 1) * T], zeros[:], 0.0,
                                                 ALU.add, ALU.add).then_inc(run_done[u], 1)
                dve.wait_ge(run_done[u], 2 * p + 2)
                for j in range(2):
                    i = nc.vector.scalar_tensor_tensor(
                        out=hid[:, u, j * T:(j + 1) * T], in0=decay[:, u, j * T:(j + 1) * T],
                        scalar=vec("cond").rearrange("p (c b) -> p c b", c=DC)[:, u, bass.ds(2 * p + j, 1)],
                        in1=hid[:, u, j * T:(j + 1) * T], op0=ALU.mult, op1=ALU.add)
                    i.then_inc((dve_step, hid_ready[u])[j], 1)
            flow(dve, first, second, third)


JOBS = {
    0: [(0, 2, 0, T, 0, T), (2, 2, 0, T, 0, T)],
    1: [(0, 4, 0, SEG[0][1] + 1, 0, SEG[0][1]), (0, 4, SEG[2][0], T, SEG[2][0], T)],
    2: [(0, 2, SEG[1][0] - 1, T, SEG[1][0], T), (2, 2, SEG[1][0] - 1, T, SEG[1][0], T)],
    3: [(0, 2, 0, T, 0, T), (2, 2, 0, T, 0, T)],
}
KEPT = [[0, 1, 3], [0, 2, 3], [0, 1, 2, 3]]
CH = 16
NCH = T // CH


def experts(nc, env):
    fp32, fp32r, ALU, ACT, AX = (env[k] for k in ("fp32", "fp32r", "ALU", "ACT", "AX"))
    sb, ps, sem, vec = (env[k] for k in ("sb", "ps", "sem", "vec"))
    XT, silu = env["XT"], env["silu"]
    st = ExitStack()
    with st:
        xhi = sb(st, "xhi", [P, DC, B, T], fp32r)
        xlo = sb(st, "xlo", [P, DC, B, T], fp32r)
        w1 = sb(st, "w1", [P, 2, 2, DC, F], fp32r)
        w2 = sb(st, "w2", [P, 2, 2, FC, D], fp32r)
        g = sb(st, "g", [P, 2, 2 * T])
        ghi = sb(st, "ghi", [P, 2, 2 * T], fp32r)
        glo = sb(st, "glo", [P, 2, 2 * T], fp32r)
        dve_step, pool_step = sem(st, "dve_step3"), sem(st, "pool_step3")
        w_split = sem(st, "w_split")
        up_done, gelu_done, hi_done, lo_done, down_done = ([sem(st, f"{n}{q}") for q in range(2)] for n in
                                                           ("up_done", "gelu_done", "hi_done", "lo_done", "down_done"))
        y_free = sem(st, "y_free")

        def products(pe, dst, whi, wlo, hi, lo, first, last):
            out = []
            for n, (w, x) in enumerate(((whi, hi), (whi, lo), (wlo, hi))):
                out.append(lambda w=w, x=x, n=n: nc.tensor.matmul(dst, w, x, start=(first and n == 0), stop=(last and n == 2)))
            return out

        def up(pe, ph, buf, f, xs, n):
            out = []
            for c in range(DC):
                w = [w1[:, buf, k, c, f * P:(f + 1) * P] for k in range(2)]
                out += products(pe, ph[f % 2][:, 0:n], w[0], w[1], xhi[:, c][xs], xlo[:, c][xs], c == 0, c == DC - 1)
            return out

        def down(pe, py, buf, f, n):
            out = []
            for m in range(DC):
                w = [w2[:, buf, k, f, m * P:(m + 1) * P] for k in range(2)]
                out += products(pe, py[:, m, 0:n], w[0], w[1], ghi[:, f % 2, 0:n], glo[:, f % 2, 0:n], f == 0, f == FC - 1)
            return out

        def split_hidden(dve, f, m, n):
            q = f % 2
            dve.wait_ge(gelu_done[q], m + 1)
            dve.wait_ge(down_done[q], m)
            nc.vector.tensor_copy(ghi[:, q, 0:n], g[:, q, 0:n]).then_inc(hi_done[q], 1)
            dve.wait_ge(hi_done[q], m + 1)
            nc.vector.tensor_tensor(glo[:, q, 0:n], g[:, q, 0:n], ghi[:, q, 0:n].bitcast(fp32), ALU.subtract).then_inc(lo_done[q], 1)

        def gelu(act, ph, bias, f, m, n):
            q = f % 2
            act.wait_ge(up_done[q], m + 1)
            act.wait_ge(lo_done[q], m)
            nc.scalar.activation(g[:, q, 0:n], ph[q][:, 0:n], ACT.Gelu_apprx_tanh, bias=bias).then_inc(gelu_done[q], 1)

        with ExitStack() as routed:
            raw1 = sb(routed, "raw1", [P, DC, F])
            raw2 = sb(routed, "raw2", [P, FC, D])
            segs = sb(routed, "segs", [P, 3, DC, B])
            agg = sb(routed, "agg", [P, 3, DC, B])
            prod = sb(routed, "prod", [P, 3 * DC, B, NE])
            prod2 = sb(routed, "prod2", [P, DC, B, 2 * NE])
            ones = sb(routed, "ones", [P, P])
            earlier = sb(routed, "earlier", [P, NE, NE])
            lg = sb(routed, "lg", [P, B, NE])
            md = sb(routed, "md", [P, B, 2 * NE])
            red = sb(routed, "red", [P, B])
            gt = sb(routed, "gt", [P, B, NE, NE])
            eq = sb(routed, "eq", [P, B, NE, NE])
            we = sb(routed, "we", [P, B, NE])
            bt = sb(routed, "bt", [P, DC, B, 3])
            ph = [ps(routed, f"ph{q}", [P, 512]) for q in range(2)]
            py = [ps(routed, f"py{q}", [P, DC, 512]) for q in range(2)]
            pgate = ps(routed, "pgate", [P, B * NE])
            ptime = ps(routed, "ptime", [P, 2 * NE * B])
            raw_in1, raw_in2, raw_used1, raw_used2, hi_copied = (sem(routed, n) for n in
                                                                 ("raw_in1", "raw_in2", "raw_used1", "raw_used2", "hi_copied"))
            gate_in, gate_mm, exp_in, exp_done, x_hi, x_split, tables = (
                sem(routed, n) for n in ("gate_in", "gate_mm", "exp_in", "exp_done", "x_hi", "x_split", "tables"))
            w_used = sem(routed, "w_used")
            block = routed.enter_context(nc.Block())
            ROUNDS = 4

            @block.sync
            def _(sp):
                for signal in up_done + gelu_done + hi_done + lo_done + down_done + [y_free]:
                    sp.sem_inc(signal, PRIMED)
                for e in range(NE + 1):
                    a, b = (env["ew1"][e], env["ew2"][e]) if e < NE else (env["sw1"], env["sw2"])
                    if e > 0:
                        sp.wait_ge(raw_used1, 2 * e)
                    sp.dma_start(raw1[:], a.rearrange("(c p) f -> p c f", p=P)).then_inc(raw_in1, 16)
                    if e > 0:
                        sp.wait_ge(raw_used2, 2 * e)
                    sp.dma_start(raw2[:], b.rearrange("(c p) d -> p c d", p=P)).then_inc(raw_in2, 16)

            @block.gpsimd
            def _(pool):
                nc.gpsimd.memset(ones[:], 1.0).then_inc(tables, 1)
                nc.gpsimd.memset(earlier[:], 0.0).then_inc(tables, 1)
                pool.wait_ge(tables, 2)
                for e in range(1, NE):
                    nc.gpsimd.memset(earlier[:, e, 0:e], 1.0).then_inc(tables, 1)

                def split_weights(e):
                    for w, raw, arrived, used in ((w1, raw1, raw_in1, raw_used1), (w2, raw2, raw_in2, raw_used2)):
                        pool.wait_ge(arrived, 16 * (e + 1))
                        if e >= 2:
                            pool.wait_ge(w_used, e - 1)
                        nc.gpsimd.tensor_copy(w[:, e % 2, 0], raw[:]).then_inc(used, 1)
                        pool.wait_ge(used, 2 * e + 1)
                        nc.gpsimd.tensor_tensor(w[:, e % 2, 1], raw[:], w[:, e % 2, 0].bitcast(fp32), ALU.subtract).then_inc(used, 1)
                    pool.wait_ge(raw_used1, 2 * e + 2)
                    pool.wait_ge(raw_used2, 2 * e + 2)
                    pool.sem_inc(w_split, 1)

                split_weights(0)
                for c in range(DC):
                    pool.wait_ge(x_hi, c + 1)
                    nc.gpsimd.tensor_tensor(xlo[:, c], XT[:, c], xhi[:, c].bitcast(fp32), ALU.subtract).then_inc(x_split, 1)
                for e in range(1, NE + 1):
                    split_weights(e)

            @block.scalar
            def _(act):
                act.wait_ge(exp_in, 1)
                nc.scalar.activation(lg[:], lg[:], ACT.Exp).then_inc(exp_done, 1)
                for e in range(NE):
                    with act.Fori(0, ROUNDS) as i:
                        for s in range(2):
                            _, nb, t0, t1, _, _ = JOBS[e][s]
                            for f in range(FC):
                                m = PRIMED + ((e * ROUNDS * 2 + s) * FC + f) // 2 + i * FC
                                gelu(act, ph, vec("eb1", e * FC + f, e * FC + f + 1), f, m, nb * (t1 - t0))

            @block.vector
            def _(dve):
                s = Steps(dve, dve_step)
                for c in range(DC):
                    nc.vector.tensor_copy(xhi[:, c], XT[:, c]).then_inc(x_hi, 1)
                for n, (a, z) in enumerate(SEG):
                    for c in range(DC):
                        s.op(nc.vector.reduce_sum(segs[:, n, c], XT[:, c, :, a:z], AX.X))
                s.fence()
                s.op(nc.vector.tensor_tensor(agg[:, 1], segs[:, 0], segs[:, 2], ALU.add))
                s.link(nc.vector.tensor_tensor(agg[:, 2], segs[:, 1], segs[:, 2], ALU.add))
                s.link(nc.vector.tensor_tensor(agg[:, 0], agg[:, 1], segs[:, 1], ALU.add))
                sizes = [z - a for a, z in SEG]
                for n, count in enumerate((T, sizes[0] + sizes[2], sizes[1] + sizes[2])):
                    s.op(nc.vector.tensor_scalar(agg[:, n], agg[:, n], 1.0 / count, None, ALU.mult))
                s.fence()
                s.op(nc.vector.tensor_tensor(prod[:], agg[:].rearrange("p n c b -> p (n c) b").unsqueeze(3).broadcast_to([P, 3 * DC, B, NE]),
                                             vec("gate_w").rearrange("p (k e) -> p k e", e=NE).unsqueeze(2).broadcast_to([P, 3 * DC, B, NE]),
                                             ALU.mult))
                nc.vector.tensor_tensor(prod2[:], silu[:].unsqueeze(3).broadcast_to([P, DC, B, 2 * NE]),
                                        vec("time_w").rearrange("p (k e) -> p k e", e=2 * NE).unsqueeze(2).broadcast_to([P, DC, B, 2 * NE]),
                                        ALU.mult).then_inc(gate_in, 1)
                dve.wait_ge(gate_mm, 1)
                s.op(nc.vector.tensor_tensor(lg[:], pgate[:].rearrange("p (b e) -> p b e", e=NE),
                                             vec("gate_b").unsqueeze(1).broadcast_to([P, B, NE]), ALU.add))
                s.link(nc.vector.tensor_tensor(md[:], ptime[:].rearrange("p (b e) -> p b e", e=2 * NE),
                                               vec("time_b").unsqueeze(1).broadcast_to([P, B, 2 * NE]), ALU.add))
                s.link(nc.vector.scalar_tensor_tensor(out=lg[:], in0=md[:, :, 0:NE], scalar=1.0, in1=lg[:], op0=ALU.add, op1=ALU.mult))
                s.link(nc.vector.tensor_tensor(lg[:], lg[:], md[:, :, NE:2 * NE], ALU.add))
                s.link(nc.vector.reduce_max(red[:], lg[:], AX.X))
                nc.vector.tensor_tensor(lg[:], lg[:], red[:].unsqueeze(2).broadcast_to([P, B, NE]), ALU.subtract).then_inc(exp_in, 1)
                dve.wait_ge(exp_done, 1)
                s.link(nc.vector.reduce_sum(red[:], lg[:], AX.X))
                s.link(nc.vector.reciprocal(red[:], red[:]))
                s.link(nc.vector.tensor_tensor(lg[:], lg[:], red[:].unsqueeze(2).broadcast_to([P, B, NE]), ALU.mult))
                mine = lg[:].unsqueeze(3).broadcast_to([P, B, NE, NE])
                other = lg[:].unsqueeze(2).broadcast_to([P, B, NE, NE])
                s.op(nc.vector.tensor_tensor(gt[:], other, mine, ALU.is_gt))
                s.link(nc.vector.tensor_tensor(eq[:], other, mine, ALU.is_equal))
                dve.wait_ge(tables, 5)
                s.link(nc.vector.tensor_tensor(eq[:], eq[:], earlier[:].unsqueeze(1).broadcast_to([P, B, NE, NE]), ALU.mult))
                s.link(nc.vector.tensor_tensor(gt[:], gt[:], eq[:], ALU.add))
                s.link(nc.vector.reduce_sum(we[:], gt[:], AX.X))
                s.link(nc.vector.tensor_scalar(we[:], we[:], 1.5, None, ALU.is_lt))
                s.link(nc.vector.tensor_tensor(we[:], we[:], lg[:], ALU.mult))
                s.link(nc.vector.reduce_sum(red[:], we[:], AX.X))
                s.link(nc.vector.tensor_scalar(red[:], red[:], 1e-8, None, ALU.add))
                s.link(nc.vector.reciprocal(red[:], red[:]))
                s.link(nc.vector.tensor_tensor(we[:], we[:], red[:].unsqueeze(2).broadcast_to([P, B, NE]), ALU.mult))
                for n in range(4):
                    for k, seen in enumerate(KEPT):
                        if n >= len(seen):
                            continue
                        e = seen[n]
                        for c in range(DC):
                            bias = vec("eb2", e * DC + c, e * DC + c + 1)
                            if n == 0:
                                s.op(nc.vector.tensor_scalar(bt[:, c, :, k], we[:, :, e], bias, vec("sb2", c, c + 1), ALU.mult, ALU.add))
                            else:
                                s.op(nc.vector.scalar_tensor_tensor(out=bt[:, c, :, k], in0=we[:, :, e], scalar=bias,
                                                                    in1=bt[:, c, :, k], op0=ALU.mult, op1=ALU.add))
                    s.fence()
                dve.wait_ge(x_split, DC)
                for c in range(DC):
                    for k, (a, z) in enumerate(SEG):
                        s.op(nc.vector.tensor_tensor(XT[:, c, :, a:z], XT[:, c, :, a:z],
                                                     bt[:, c, :, k:k + 1].broadcast_to([P, B, z - a]), ALU.add))
                s.fence()
                at = s.n
                for e in range(NE):
                    each = sum(job[1] for job in JOBS[e])
                    with dve.Fori(0, ROUNDS) as i:
                        done = 0
                        for s_ in range(2):
                            b0, nb, t0, t1, k0, k1 = JOBS[e][s_]
                            n = nb * (t1 - t0)
                            for f in range(FC):
                                m = PRIMED + ((e * ROUNDS * 2 + s_) * FC + f) // 2 + i * FC
                                split_hidden(dve, f, m, n)
                            dve.wait_ge(down_done[(FC - 1) % 2], m + 1)
                            for b in range(nb):
                                xv = XT[:, :, bass.ds(4 * i + (b0 + b), 1), k0:k1].rearrange("p c o t -> p c (o t)")
                                y0 = b * (t1 - t0) + k0 - t0
                                ins = nc.vector.scalar_tensor_tensor(
                                    out=xv, in0=py[s_][:, :, y0:y0 + k1 - k0],
                                    scalar=we[:].rearrange("p b e -> p e b")[:, e, bass.ds(4 * i + (b0 + b), 1)], in1=xv,
                                    op0=ALU.mult, op1=ALU.add)
                                ins.then_inc(y_free if b == nb - 1 else dve_step, 1)
                    dve.wait_ge(y_free, PRIMED + 2 * (e + 1) * ROUNDS)

            @block.tensor
            def _(pe):
                pe.wait_ge(gate_in, 1)
                pe.wait_ge(tables, 1)
                for k in range(3 * DC):
                    nc.tensor.matmul(pgate[:], ones[:], prod[:, k].rearrange("p b e -> p (b e)"), start=(k == 0), stop=(k == 3 * DC - 1))
                for k in range(DC):
                    i = nc.tensor.matmul(ptime[:], ones[:], prod2[:, k].rearrange("p b e -> p (b e)"), start=(k == 0), stop=(k == DC - 1))
                i.then_inc(gate_mm, 1)
                pe.wait_ge(x_split, DC)
                for e in range(NE):
                    pe.wait_ge(w_split, e + 1)
                    with pe.Fori(0, ROUNDS) as i:
                        for s in range(2):
                            b0, nb, t0, t1, _, _ = JOBS[e][s]
                            n, xs = nb * (t1 - t0), (slice(None), bass.ds(4 * i + b0, nb), slice(t0, t1))

                            def issue(ops, done):
                                for o in ops:
                                    ins = o()
                                ins.then_inc(done, 1)
                            for f in range(FC + 1):
                                if f < FC:
                                    m = PRIMED + ((e * ROUNDS * 2 + s) * FC + f) // 2 + i * FC
                                    pe.wait_ge(gelu_done[f % 2], m)
                                    issue(up(pe, ph, e % 2, f, xs, n), up_done[f % 2])
                                if f > 0:
                                    m = PRIMED + ((e * ROUNDS * 2 + s) * FC + f - 1) // 2 + i * FC
                                    pe.wait_ge(lo_done[(f - 1) % 2], m + 1)
                                    if f == 1:
                                        prior = 2 * (e * ROUNDS + i) + s - 1
                                        pe.wait_ge(y_free, PRIMED + (prior if not (e == 0 and s == 0) else 2 * i))
                                    issue(down(pe, py[s], e % 2, f - 1, n), down_done[(f - 1) % 2])
                    pe.wait_ge(down_done[1], PRIMED + (e + 1) * ROUNDS * FC)
                    pe.sem_inc(w_used, 1)

        shared_and_rnn(nc, env, locals())


def shared_and_rnn(nc, env, ex):
    fp32, ALU, ACT = (env[k] for k in ("fp32", "ALU", "ACT"))
    sb, ps, sem, vec = (env[k] for k in ("sb", "ps", "sem", "vec"))
    XT, wx, wh, out = (env[k] for k in ("XT", "wx_sb", "wh_sb", "out"))
    up, down, gelu, split_hidden = (ex[k] for k in ("up", "down", "gelu", "split_hidden"))
    up_done, gelu_done, lo_done, down_done = (ex[k] for k in ("up_done", "gelu_done", "lo_done", "down_done"))
    N = B * CH
    BUF = NE % 2
    EACH = 2 * FC * 6 // CH
    M0 = PRIMED + NE * 4 * FC
    st = ExitStack()
    with st:
        hs = sb(st, "hs", [P, 2, CH, DC, B])
        staged = sb(st, "staged", [P, 2, DC, B, CH])
        ones = sb(st, "ones_row", [1, N])
        ph = [ps(st, f"phs{q}", [P, 512]) for q in range(2)]
        py = ps(st, "pys", [P, DC, 512])
        pr = [ps(st, f"pr{q}", [P, DC, 512 // B, B]) for q in range(2)]
        ones_set, half_added, x_ready, step_done, tanh_done = (
            sem(st, n) for n in ("ones_set", "half_added", "x_ready", "step_done", "tanh_done"))
        staged_done, out_done = ([sem(st, f"{n}{s}") for s in range(2)] for n in ("staged_done", "out_done"))
        block = st.enter_context(nc.Block())

        def chunk_loop(eng, chunk, recur, last):
            chunk(0, 0, None)
            with eng.Fori(0, NCH // 2 - 1) as i:
                chunk(2 * i + 1, 1, i)
                chunk(2 * i + 2, 0, i)
            chunk(NCH - 1, 1, NCH // 2 - 1)
            for k in range(CH):
                recur(NCH // 2 - 1, 1, k)
            last(NCH // 2 - 1, 1)

        def steps_by(f):
            return 0 if f < 0 else CH // FC // 2 if f == 0 else CH // FC * f if f < FC else CH

        @block.tensor
        def _(pe):
            def recur(q, s, k):
                pe.wait_ge(tanh_done, PRIMED + CH * (2 * q + s) + k)
                prev = hs[:, s, k - 1] if k > 0 else hs[:, 1 - s, CH - 1]
                for m in range(DC):
                    for c in range(DC):
                        i = nc.tensor.matmul(pr[s][:, m, k], wh[:, c, m * P:(m + 1) * P], prev[:, c],
                                             start=False, stop=(c == DC - 1), skip_group_check=True)
                i.then_inc(step_done, 1)

            def chunk(c, s, q):
                xs = (slice(None), slice(0, B), bass.ds(CH * c, CH))
                steps = list(range(CH))

                def spread(ops, done):
                    for n, o in enumerate(ops):
                        ins = o()
                        if n == len(ops) - 1:
                            ins.then_inc(done, 1)
                        if n % EACH == EACH - 1 and q is not None:
                            recur(q, 1 - s, steps.pop(0))
                for f in range(FC + 1):
                    if f < FC:
                        pe.wait_ge(gelu_done[f % 2], M0 + c * (FC // 2) + f // 2)
                        spread(up(pe, ph, BUF, f, xs, N), up_done[f % 2])
                    if f > 0:
                        pe.wait_ge(lo_done[(f - 1) % 2], M0 + c * (FC // 2) + (f - 1) // 2 + 1)
                        if f == 1:
                            pe.wait_ge(x_ready, c)
                        spread(down(pe, py, BUF, f - 1, N), down_done[(f - 1) % 2])
                assert q is None or not steps
                pe.wait_ge(x_ready, c + 1)
                for m in range(DC):
                    dst = pr[s][:, m, 0:CH].rearrange("p t b -> p (t b)")
                    nc.tensor.matmul(dst, vec("rnn_b_row")[0:1, m * P:(m + 1) * P], ones[:, :], start=True, stop=False)
                    for k in range(DC):
                        nc.tensor.matmul(dst, wx[:, k, m * P:(m + 1) * P],
                                         XT[:, k, :, bass.ds(CH * c, CH)].rearrange("p b t -> p t b"), start=False, stop=(k == DC - 1))
            pe.wait_ge(ones_set, 2)
            chunk_loop(pe, chunk, recur, lambda r, s: None)

        @block.scalar
        def _(act):
            def recur(q, s, k):
                act.wait_ge(step_done, CH * (2 * q + s) + k + 1)
                if k == 0:
                    act.wait_ge(staged_done[s], PRIMED + q)
                nc.scalar.activation(hs[:, s, k], pr[s][:, :, k], ACT.Tanh).then_inc(tanh_done, 1)

            def chunk(c, s, q):
                for f in range(FC + 1):
                    if q is not None:
                        for k in range(steps_by(f - 1), steps_by(f)):
                            recur(q, 1 - s, k)
                    if f < FC:
                        gelu(act, ph, vec("sb1", f, f + 1), f, M0 + c * (FC // 2) + f // 2, N)
            chunk_loop(act, chunk, recur, lambda r, s: None)

        @block.vector
        def _(dve):
            nc.vector.memset(ones[:, :], 1.0).then_inc(ones_set, 1)
            nc.vector.tensor_copy(hs[:, 1, CH - 1], vec("cond").rearrange("p (c b) -> p c b", c=DC)).then_inc(ones_set, 1)

            def stage(q, s):
                r = 2 * q + s
                dve.wait_ge(tanh_done, PRIMED + CH * (r + 1))
                dve.wait_ge(out_done[s], PRIMED + 16 * q)
                nc.vector.tensor_tensor(staged[:, s], XT[:, :, :, bass.ds(CH * r, CH)],
                                        hs[:, s].rearrange("p t c b -> p c b t"), ALU.add).then_inc(staged_done[s], 1)

            def chunk(c, s, q):
                for f in range(FC):
                    split_hidden(dve, f, M0 + c * (FC // 2) + f // 2, N)
                dve.wait_ge(down_done[(FC - 1) % 2], M0 + c * (FC // 2) + FC // 2)
                for m in range(DC):
                    xv = XT[:, m, :, bass.ds(CH * c, CH)]
                    i = nc.vector.tensor_tensor(xv, xv, py[:, m, 0:N].rearrange("p (b t) -> p b t", b=B), ALU.add)
                    i.then_inc(half_added if m == 0 else x_ready, 1)
                if q is not None:
                    stage(q, 1 - s)
            chunk_loop(dve, chunk, lambda r, s, k: None, stage)

        @block.sync
        def _(sp):
            def send(q, s):
                c = 2 * q + s
                sp.wait_ge(staged_done[s], PRIMED + q + 1)
                sp.dma_start(out[bass.ds(c, 1)].rearrange("o p n -> p (o n)"), staged[:, s].rearrange("p c b t -> p (c b t)")).then_inc(out_done[s], 16)
            for signal in [tanh_done] + staged_done + out_done:
                sp.sem_inc(signal, PRIMED)
            with sp.Fori(0, NCH // 2) as i:
                send(i, 0)
                send(i, 1)
            for s in range(2):
                sp.wait_ge(out_done[s], PRIMED + 16 * (NCH // 2))


_INS = ["x_tok", "x_dm", "small", "mod_w", "w_qkv", "w_out", "w_fih", "ew1", "ew2", "sw1", "sw2", "wx", "wh"]


def kernel(x, cond_1024, L0_cond_position, L0_cond_mod_w, L0_cond_mod_b, L0_cond_w_qkv, L0_cond_w_out,
           L0_cond_q_norm_w, L0_cond_k_norm_w, L1_cond_W_f, L1_cond_b_f, L1_cond_W_i, L1_cond_b_i, L1_cond_W_h,
           L1_cond_b_h, L2_cond_gate_w, L2_cond_gate_b, L2_cond_time_w, L2_cond_time_b, L2_cond_ew1, L2_cond_eb1,
           L2_cond_ew2, L2_cond_eb2, L2_cond_sw1, L2_cond_sb1, L2_cond_sw2, L2_cond_sb2, L3_cond_Wx, L3_cond_Wh,
           L3_cond_b):
    import numpy as np
    import concourse.bacc as bacc
    from concourse import mybir as mb
    from concourse.bass_utils import run_bass_kernel_spmd

    def columns(v):
        return np.reshape(np.asarray(v), (-1, P)).T

    def rows(w):
        w = np.asarray(w)
        return w.reshape(-1, P, w.shape[-1]).transpose(1, 0, 2).reshape(P, -1)

    def everywhere(*vs):
        v = np.concatenate([np.ravel(np.asarray(v)) for v in vs])
        return np.broadcast_to(v, (P, v.size))

    parts = {
        "mod_b": columns(L0_cond_mod_b), "b_f": columns(L1_cond_b_f), "b_i": columns(L1_cond_b_i),
        "b_h": columns(L1_cond_b_h), "eb1": columns(L2_cond_eb1), "sb1": columns(L2_cond_sb1),
        "eb2": columns(L2_cond_eb2), "sb2": columns(L2_cond_sb2), "rnn_b": columns(L3_cond_b),
        "cond": rows(np.asarray(cond_1024).T), "qk_w": everywhere(L0_cond_q_norm_w, L0_cond_k_norm_w),
        "gate_b": everywhere(L2_cond_gate_b), "time_b": everywhere(L2_cond_time_b), "gate_w": rows(L2_cond_gate_w),
        "time_w": rows(L2_cond_time_w), "pos": rows(np.asarray(L0_cond_position).reshape(T, ROT)), "rnn_b_row": everywhere(L3_cond_b),
    }
    xs = np.asarray(x)
    arrays = {
        "x_tok": xs, "x_dm": xs.transpose(2, 0, 1), "small": np.concatenate([parts[n] for n, _ in SMALL], axis=1),
        "mod_w": L0_cond_mod_w, "w_qkv": L0_cond_w_qkv, "w_out": L0_cond_w_out,
        "w_fih": np.concatenate([np.asarray(w).T for w in (L1_cond_W_f, L1_cond_W_i, L1_cond_W_h)], axis=1),
        "ew1": L2_cond_ew1, "ew2": L2_cond_ew2, "sw1": L2_cond_sw1, "sw2": L2_cond_sw2, "wx": L3_cond_Wx, "wh": L3_cond_Wh,
    }
    arrays = {n: np.ascontiguousarray(a) for n, a in arrays.items()}
    nc = bacc.Bacc("TRN2", target_bir_lowering=False, num_devices=1)
    args = [nc.dram_tensor("in_" + n, arrays[n].shape, mb.dt.from_np(arrays[n].dtype), kind="ExternalInput").ap() for n in _INS]
    out = nc.dram_tensor("out_dm", (NCH, P, DC * B * CH), mb.dt.float32, kind="ExternalOutput").ap()
    build(nc, *args, out)
    r = run_bass_kernel_spmd(nc, [{"in_" + n: a for n, a in arrays.items()}], core_ids=[0])
    o = np.asarray(r.results[0]["out_dm"]).reshape(NCH, P, DC, B, CH)
    return np.ascontiguousarray(o.transpose(3, 0, 4, 2, 1).reshape(B, T, D))
```
